# Optimizing a Trainium2 kernel written in Bass

```python
import numpy as np
import jax
import jax.numpy as jnp

def _softmax(x, axis=-1):
    return jax.nn.softmax(x, axis=axis)

def _gelu(x):
    return jax.nn.gelu(x, approximate=True)

def _silu(x):
    return jax.nn.silu(x)

def _sigmoid(x):
    return jax.nn.sigmoid(x)

def _layernorm(x, axis=-1, eps=1e-05):
    m = jnp.mean(x, axis=axis, keepdims=True)
    v = jnp.var(x, axis=axis, keepdims=True)
    return (x - m) / jnp.sqrt(v + eps)

def _scatter_add(tgt, idx, src, axis=0):
    return tgt.at[idx].add(src)

def _segment_sum(src, seg, n):
    return jax.ops.segment_sum(src, seg, n)
kernel_name = 'mk_early_fusion_d1_tok_img4096_r4_e42c46'

def setup_inputs(seed: int=0):
    np.random.seed(seed)
    _w = jnp.asarray

    def _rec_inputs():
        import jax
        import jax.numpy as jnp
        _rk = jax.random.key(seed)
        x = -0.0064186 + 0.999588 * jax.random.normal(jax.random.fold_in(_rk, 1), (32, 128, 64, 2), jnp.float32)
        txt = 0.000163725 + 0.02 * jax.random.normal(jax.random.fold_in(_rk, 2), (32, 77, 1024), jnp.float32)
        return (x, txt)
    x, txt = _rec_inputs()

    def _L0_tok_setup():
        import jax, jax.numpy as jnp
        import numpy as np
        import math
        H, N, C, L_VAL = (128, 64, 1, 1024)
        EPS = 1e-07

        def _reciprocal(x, epsilon):
            xc = jnp.conj(x)
            return xc / (x * xc + epsilon)
        key = jax.random.key(seed)
        k1, k2, k3 = jax.random.split(key, 3)
        log_dt = math.log(0.001) + jax.random.uniform(k1, (H,), dtype=jnp.float32) * (math.log(0.1) - math.log(0.001))
        log_dt = jnp.tile(log_dt[:, None], (1, 2))
        lam_im = jax.random.normal(k2, (N,), dtype=jnp.float32)
        Lambda = jnp.stack([-0.5 * jnp.ones((N,), jnp.float32), lam_im], axis=-1)
        W = jax.random.normal(k3, (C, H, N, 2), dtype=jnp.float32)
        return {'log_dt': log_dt, 'Lambda': Lambda, 'W': W, 'L': L_VAL}
    _L0_tok_all = _L0_tok_setup()
    _L0_tok_in = {k: v for k, v in _L0_tok_all.items() if k in ('log_dt', 'Lambda')}
    del _L0_tok_all

    def _L0_attn_setup():
        import jax, jax.numpy as jnp
        import numpy as np
        B, S, D = (2, 512, 1024)
        NH, NKV = (32, 8)
        HD = D // NH
        NREP = NH // NKV
        SCALE = HD ** (-0.5)
        key = jax.random.key(seed)
        kx, kq, kk, kv, ko = jax.random.split(key, 5)
        s = 0.02
        return {'x': jax.random.normal(kx, (B, S, D), dtype=jnp.float32), 'wq': jax.random.normal(kq, (D, NH * HD), dtype=jnp.float32) * s, 'wk': jax.random.normal(kk, (D, NKV * HD), dtype=jnp.float32) * s, 'wv': jax.random.normal(kv, (D, NKV * HD), dtype=jnp.float32) * s, 'wo': jax.random.normal(ko, (NH * HD, D), dtype=jnp.float32) * s}
    _L0_attn_all = _L0_attn_setup()
    _L0_attn_in = {k: v for k, v in _L0_attn_all.items() if k in ('wq', 'wk', 'wv', 'wo')}
    del _L0_attn_all

    def _L0_ffn_setup():
        import math
        import jax, jax.numpy as jnp
        import numpy as np
        SCALING = 16.0 / 32.0

        def real_fourier_orthogonal_multiply(c):
            n = c.shape[-1]
            sqrt_n = math.sqrt(n)
            pair_scale = math.sqrt(n / 2.0)
            max_f = (n - 1) // 2
            work = c.astype(jnp.float32)
            dc = (work[..., 0] * sqrt_n)[..., None].astype(jnp.complex64)
            cos = work[..., 1:1 + 2 * max_f:2] * pair_scale
            sin = work[..., 2:2 + 2 * max_f:2] * pair_scale
            mid = (cos - 1j * sin).astype(jnp.complex64)
            parts = [dc, mid]
            if n % 2 == 0:
                parts.append((work[..., -1] * sqrt_n)[..., None].astype(jnp.complex64))
            spectrum = jnp.concatenate(parts, axis=-1)
            return jnp.fft.irfft(spectrum, n=n, axis=-1).astype(c.dtype)
        key = jax.random.key(seed)
        ks = jax.random.split(key, 9)
        B, S, D_in, D_out, R0, R1, E = (4, 512, 1024, 1024, 32, 8, 3)
        x = jax.random.normal(ks[0], (B, S, D_in), dtype=jnp.float32)
        W_base = jax.random.normal(ks[1], (D_out, D_in), dtype=jnp.float32) * 0.02
        b_base = jax.random.normal(ks[2], (D_out,), dtype=jnp.float32) * 0.02
        enc0 = jax.random.normal(ks[3], (R0, D_in), dtype=jnp.float32) * 0.02
        enc1 = jax.random.normal(ks[4], (R1, D_in), dtype=jnp.float32) * 0.02
        coefs0 = jax.random.normal(ks[5], (E, D_out, R0), dtype=jnp.float32) * 0.02
        coefs1 = jax.random.normal(ks[6], (E, D_out, R1), dtype=jnp.float32) * 0.02
        mask0 = jax.random.randint(ks[7], (E, D_out, R0), 0, 2).astype(bool)
        mask1 = jax.random.randint(ks[8], (E, D_out, R1), 0, 2).astype(bool)
        return dict(x=x, W_base=W_base, b_base=b_base, enc0=enc0, enc1=enc1, coefs0=coefs0, coefs1=coefs1, mask0=mask0, mask1=mask1)
    _L0_ffn_all = _L0_ffn_setup()
    _L0_ffn_in = {k: v for k, v in _L0_ffn_all.items() if k in ('W_base', 'b_base', 'enc0', 'enc1', 'coefs0', 'coefs1', 'mask0', 'mask1')}
    del _L0_ffn_all
    return {'x': x, 'txt': txt, 'L0_tok_log_dt': _L0_tok_in['log_dt'], 'L0_tok_Lambda': _L0_tok_in['Lambda'], 'L0_attn_wq': _L0_attn_in['wq'], 'L0_attn_wk': _L0_attn_in['wk'], 'L0_attn_wv': _L0_attn_in['wv'], 'L0_attn_wo': _L0_attn_in['wo'], 'L0_ffn_W_base': _L0_ffn_in['W_base'], 'L0_ffn_b_base': _L0_ffn_in['b_base'], 'L0_ffn_enc0': _L0_ffn_in['enc0'], 'L0_ffn_enc1': _L0_ffn_in['enc1'], 'L0_ffn_coefs0': _L0_ffn_in['coefs0'], 'L0_ffn_coefs1': _L0_ffn_in['coefs1'], 'L0_ffn_mask0': _L0_ffn_in['mask0'], 'L0_ffn_mask1': _L0_ffn_in['mask1']}

def reference(x, txt, L0_tok_log_dt, L0_tok_Lambda, L0_attn_wq, L0_attn_wk, L0_attn_wv, L0_attn_wo, L0_ffn_W_base, L0_ffn_b_base, L0_ffn_enc0, L0_ffn_enc1, L0_ffn_coefs0, L0_ffn_coefs1, L0_ffn_mask0, L0_ffn_mask1):
    import jax
    import jax.numpy as jnp

    def _L0_tok_ref(log_dt, Lambda, W, L):
        import jax, jax.numpy as jnp
        import numpy as np
        import math
        H, N, C, L_VAL = (128, 64, 1, 1024)
        EPS = 1e-07

        def _reciprocal(x, epsilon):
            xc = jnp.conj(x)
            return xc / (x * xc + epsilon)
        Lam = Lambda[:, 0] + 1j * Lambda[:, 1]
        Wc = W[..., 0] + 1j * W[..., 1]
        dt = jnp.exp(log_dt)
        dt_Lambda = dt[:, None, 0] * Lambda[None, :, 0] + 1j * (dt[:, None, 1] * Lambda[None, :, 1])
        pos = jnp.arange(L, dtype=jnp.float32)
        gt0 = (Lam.real > 0).astype(dt_Lambda.real.dtype)
        P_max = jax.lax.stop_gradient(dt_Lambda * (gt0 * (L - 1)))
        dt_Lambda_neg = dt_Lambda * (1 - 2 * gt0)
        num = jnp.exp(dt_Lambda_neg) - 1
        den = jnp.exp(dt_Lambda_neg * L) - 1
        Wc = Wc * num * _reciprocal(den * Lam, EPS)
        P = dt_Lambda[..., None] * pos - P_max[..., None]
        K = jnp.einsum('chn,hnl->chl', Wc, jnp.exp(P))
        return K.real.astype(jnp.float32)

    def _L0_attn_ref(x, wq, wk, wv, wo):
        import jax, jax.numpy as jnp
        import numpy as np
        B, S, D = (2, 512, 1024)
        NH, NKV = (32, 8)
        HD = D // NH
        NREP = NH // NKV
        SCALE = HD ** (-0.5)
        b, s, _ = x.shape
        q = (x @ wq).reshape(b, s, NH, HD)
        k = (x @ wk).reshape(b, s, NKV, HD)
        v = (x @ wv).reshape(b, s, NKV, HD)
        k = jnp.repeat(k, NREP, axis=2)
        v = jnp.repeat(v, NREP, axis=2)
        scores = jnp.einsum('bihd,bjhd->bhij', q, k) * SCALE
        causal = jnp.tril(jnp.ones((s, s), dtype=bool))
        scores = jnp.where(causal, scores, jnp.finfo(scores.dtype).min)
        attn = jax.nn.softmax(scores, axis=-1)
        out = jnp.einsum('bhij,bjhd->bihd', attn, v)
        out = out.reshape(b, s, NH * HD)
        return out @ wo

    def _L0_ffn_ref(x, W_base, b_base, enc0, enc1, coefs0, coefs1, mask0, mask1):
        import math
        import jax, jax.numpy as jnp
        import numpy as np
        SCALING = 16.0 / 32.0

        def real_fourier_orthogonal_multiply(c):
            n = c.shape[-1]
            sqrt_n = math.sqrt(n)
            pair_scale = math.sqrt(n / 2.0)
            max_f = (n - 1) // 2
            work = c.astype(jnp.float32)
            dc = (work[..., 0] * sqrt_n)[..., None].astype(jnp.complex64)
            cos = work[..., 1:1 + 2 * max_f:2] * pair_scale
            sin = work[..., 2:2 + 2 * max_f:2] * pair_scale
            mid = (cos - 1j * sin).astype(jnp.complex64)
            parts = [dc, mid]
            if n % 2 == 0:
                parts.append((work[..., -1] * sqrt_n)[..., None].astype(jnp.complex64))
            spectrum = jnp.concatenate(parts, axis=-1)
            return jnp.fft.irfft(spectrum, n=n, axis=-1).astype(c.dtype)
        base = jnp.einsum('bsd,od->bso', x, W_base) + b_base
        e0 = jnp.einsum('bsd,rd->bsr', x, enc0)
        e1 = jnp.einsum('bsd,rd->bsr', x, enc1)
        w0 = coefs0 * mask0.astype(coefs0.dtype)
        w1 = coefs1 * mask1.astype(coefs1.dtype)
        decoded = jnp.einsum('bsr,eor->ebso', e0, w0) + jnp.einsum('bsr,eor->ebso', e1, w1)
        transformed = real_fourier_orthogonal_multiply(decoded)
        update = transformed.sum(axis=0)
        return base + update * SCALING
    h = _L0_tok_ref(L0_tok_log_dt, L0_tok_Lambda, x, 1024)
    h = jnp.concatenate([h, txt], axis=1)
    h = h + _L0_attn_ref(_layernorm(h, axis=-1), L0_attn_wq, L0_attn_wk, L0_attn_wv, L0_attn_wo)
    h = h + _L0_ffn_ref(_layernorm(h, axis=-1), L0_ffn_W_base, L0_ffn_b_base, L0_ffn_enc0, L0_ffn_enc1, L0_ffn_coefs0, L0_ffn_coefs1, L0_ffn_mask0, L0_ffn_mask1)
    return h

_drawn_inputs = setup_inputs


def setup_inputs(seed=0):
    import zlib

    import numpy as np

    out = dict(_drawn_inputs(seed))
    spreads = {}
    factors = {}
    for name, (base, spread) in spreads.items():
        noise = np.random.default_rng([zlib.crc32(name.encode()), seed]).standard_normal(out[name].shape)
        drawn = base * np.exp(spread * noise) if base else spread * noise
        out[name] = jnp.asarray(drawn.astype(out[name].dtype))
    for name, factor in factors.items():
        out[name] = (out[name] * factor).astype(out[name].dtype)
    return out
```

```python
from contextlib import ExitStack

import numpy as np

import concourse.bass as bass
from concourse import mybir

F32 = mybir.dt.float32
F16 = mybir.dt.float16
BF16 = mybir.dt.bfloat16
I32 = mybir.dt.int32
ALU = mybir.AluOpType
ACT = mybir.ActivationFunctionType
AX = mybir.AxisListType
RMAX = bass.bass_isa.ReduceOp.max

P = 128
B = 32
H = 128
N = 64
L = 1024
D = 1024
TXT = 77
S = H + TXT
ROWS = B * S
KC = D // P
NH, NKV, HD = 32, 8, 32
REP = NH // NKV
QW, KW = NH * HD, NKV * HD
R0, R1, E = 32, 8, 3
R = R0 + R1
ROUND = 12582912.0
TWO_PI = 6.283185
LA, LB = 4, L // 4
HC = 8
MROW = 32768.0
STACK = 3 * HD
TOP = {"q": 4.0, "k": 2.0, "o": 8.0, "f": 8.0}
EPS_LN = 1e-5


def wait(eng, sem, value):
    if isinstance(value, int) and value <= 0:
        return
    eng.wait_ge(sem, value)


class Chain:

    def __init__(self, eng, sem):
        self.eng, self.sem, self.base, self.n = eng, sem, 0, 0

    def __call__(self, ins, passed=None):
        ins.then_inc(self.sem, 1)
        self.n += 1
        self.eng.wait_ge(self.sem, self.base + self.n)
        if passed is not None:
            pass_on(self.eng, passed)


def pass_on(eng, passed):
    eng.sem_inc(passed, 1)


def ssm(nc, x, log_dt, lam, hcat):
    NCH = H // HC
    with ExitStack() as ctx:
        sb = lambda n, s, d=F32: ctx.enter_context(nc.sbuf_tensor(n, s, d))
        sem = lambda n: ctx.enter_context(nc.semaphore(n))
        x_sb = sb("x_sb", [P, B, 2 * N])
        wr = sb("wr", [P, B, H])
        wi = sb("wi", [P, B, H])
        ident = sb("ident1", [P, P])
        lam_sb = sb("lam_sb", [P, 2])
        ldt = sb("ldt", [P, H, 2])
        dt = sb("dt", [P, H, 2])
        g = sb("g", [P, 1])
        sgn = sb("sgn", [P, 1])
        lbg = sb("lbg", [P, 1])
        lag = sb("lag", [P, 1])
        phi = sb("phi", [P, 1])
        a = sb("a", [P, H])
        b = sb("b", [P, H])
        f = sb("f", [P, H])
        args = sb("args", [P, 2, 2, H])
        turns = sb("turns", [P, 3, 2 * H])
        whole = sb("whole", [P, 3, 2 * H])
        trig = sb("trig", [P, 3, 2 * H])
        ex = sb("ex", [P, 2 * H])
        th = sb("th", [P, 2 * H])
        t1 = sb("t1", [P, 2 * H])
        t2 = sb("t2", [P, 2 * H])
        em = sb("em", [P, 2, 2, H])
        cc = sb("cc", [P, 8, H])
        ilb = sb("ilb", [P, LB])
        ila = sb("ila", [P, LA])
        fla = sb("fla", [P, 2, LA, H])
        tla = sb("tla", [P, 2, LA, H])
        wla = sb("wla", [P, 2, LA, H])
        ela = sb("ela", [P, LA, H])
        gg = sb("gg", [P, 2, LA, H])
        tA = sb("tA", [P, LA, H])
        tt = sb("tt", [P, HC, LB])
        tw = sb("tw", [P, HC, LB])
        es = sb("es", [P, 2, HC, LB])
        mag = sb("mag", [P, 2, HC, LB])
        u = sb("u", [P, 2, HC, LA, B])
        u2 = sb("u2", [P, HC, LA, B])
        ob = sb("ob", [P, 2, HC, LB])
        ps = [ctx.enter_context(nc.psum_tensor(f"ps1_{i}", [P, 2, LB], F32)) for i in range(4)]
        pt = [ctx.enter_context(nc.psum_tensor(f"pt1_{i}", [P, 4, P], F32)) for i in range(2)]
        twice = [t[:].rearrange("p k j l -> p (k j l)").rearrange("p (c m) -> p c m", m=P) for t in (ob, es)]
        twice_ok = sem("twice_ok")
        in_small, in_x = sem("in_small"), sem("in_x")
        pool_c, dve_c = sem("pool_c"), sem("dve_c")
        ready, act_c = sem("ready"), sem("act_c")
        iota_ok, ident_ok = sem("iota_ok"), sem("ident_ok")
        xt_filled, xt_read = sem("xt_filled"), sem("xt_read")
        reduced, sin_ok, mag_ok, e_ok = sem("reduced"), sem("sin_ok"), sem("mag_ok"), sem("e_ok")
        u_ok, mm_done, k_read = sem("u_ok"), sem("mm_done"), sem("k_read")
        stored = [sem("stored0"), sem("stored1")]
        hview = hcat.rearrange("(c s) (la lb) -> la c s lb", s=S, lb=LB)
        block = ctx.enter_context(nc.Block())

        @block.sync
        def _(sp):
            sp.dma_start(lam_sb[0:N, :], lam).then_inc(in_small, 16)
            sp.dma_start(lam_sb[N:P, :], lam).then_inc(in_small, 16)
            sp.dma_start(ldt[:], log_dt.rearrange("(o h) t -> o h t", o=1).broadcast_to([P, H, 2])).then_inc(in_small, 16)
            sp.dma_start(x_sb[:], x.rearrange("c h n t -> h c (n t)")).then_inc(in_x, 16)
            for ch in range(NCH):
                sp.wait_ge(k_read, (ch + 1) * HC // 2)
                for la in range(LA):
                    sp.dma_start(hview[la, :, ch * HC:(ch + 1) * HC, :],
                                 ob[la * B:(la + 1) * B, ch % 2, :, :]).then_inc(stored[ch % 2], 16)
            for q in range(2):
                sp.wait_ge(stored[q], 16 * LA * NCH // 2)

        @block.gpsimd
        def _(pool):
            chain = Chain(pool, pool_c)
            pool.iota(ilb[:], pattern=[[1, LB]], base=0, channel_multiplier=0,
                      allow_small_or_imprecise_dtypes=True).then_inc(iota_ok, 1)
            pool.iota(ila[:], pattern=[[LB, LA]], base=0, channel_multiplier=0,
                      allow_small_or_imprecise_dtypes=True).then_inc(iota_ok, 1)
            chain(pool.memset(ident[:], 0.0))
            pool.affine_select(out=ident[:], in_=ident[:], compare_op=ALU.not_equal, fill=1.0, base=0,
                               pattern=[[-1, P]], channel_multiplier=1).then_inc(ident_ok, 1)
            for ch in range(NCH):
                pool.wait_ge(sin_ok, ch + 1)
                pool.wait_ge(mag_ok, ch + 1)
                pool.tensor_tensor(es[:, ch % 2], es[:, ch % 2], mag[:, ch % 2], ALU.mult).then_inc(e_ok, 1)

        @block.scalar
        def _(act):
            act.wait_ge(in_x, 16)
            for t in range(2):
                part = x_sb[:].rearrange("p c (n t) -> p c n t", t=2)[:, :, :, t]
                for k in range(2):
                    act.copy(twice[t][:, :, k * N:(k + 1) * N], part).then_inc(twice_ok, 1)
            act.wait_ge(in_small, 48)
            act.activation(dt[:], ldt[:], ACT.Exp).then_inc(act_c, 1)
            act.wait_ge(ready, 1)
            act.activation(ex[:], args[:, 0].rearrange("p k h -> p (k h)"), ACT.Exp).then_inc(act_c, 1)
            act.activation(th[:], args[:, 0].rearrange("p k h -> p (k h)"), ACT.Tanh, scale=0.5).then_inc(act_c, 1)
            act.activation(trig[:], turns[:], ACT.Sin, scale=TWO_PI).then_inc(act_c, 1)
            act.wait_ge(ready, 2)
            act.activation(tla[:], wla[:], ACT.Sin, scale=TWO_PI).then_inc(act_c, 1)
            act.activation(ela[:], fla[:, 0], ACT.Exp).then_inc(act_c, 1)

            def results(ch):
                for j in range(HC // 2):
                    n = ch * HC // 2 + j
                    act.wait_ge(mm_done, n + 1)
                    if j == 0 and ch >= 2:
                        act.wait_ge(stored[ch % 2], 16 * LA * (ch // 2))
                    act.copy(ob[:, ch % 2, 2 * j:2 * j + 2, :], ps[n % 4][:]).then_inc(k_read, 1)

            for ch in range(NCH):
                if ch >= 2:
                    act.wait_ge(mm_done, (ch - 1) * HC // 2)
                for j in range(HC):
                    h = ch * HC + j
                    m = act.activation(mag[:, ch % 2, j, :], ilb[:], ACT.Exp, scale=a[:, h:h + 1])
                m.then_inc(mag_ok, 1)
                if ch == 0:
                    act.wait_ge(xt_filled, 2 * B // 4)
                act.wait_ge(reduced, ch + 1)
                act.activation(es[:, ch % 2], tw[:], ACT.Sin, scale=TWO_PI).then_inc(sin_ok, 1)
                if ch:
                    results(ch - 1)
            results(NCH - 1)

        @block.vector
        def _(dve):
            chain = Chain(dve, dve_c)
            dve.memset(phi[0:N, :], 0.25)
            dve.memset(phi[N:P, :], 0.0)
            dve.wait_ge(in_small, 48)
            lr, li = lam_sb[:, 0:1], lam_sb[:, 1:2]
            chain(dve.tensor_scalar(g[:], lr, 0.0, None, ALU.is_gt))
            chain(dve.tensor_scalar(sgn[:], g[:], -2.0, 1.0, ALU.mult, ALU.add))
            dve.tensor_scalar(lag[:], g[:], -float(LB * (LA - 1)), None, ALU.mult)
            chain(dve.tensor_scalar(lbg[:], g[:], -float(LB - 1), None, ALU.mult))
            dve.wait_ge(iota_ok, 2)
            chain(dve.tensor_scalar(ilb[:], ilb[:], lbg[:, 0:1], None, ALU.add))
            chain(dve.tensor_scalar(ila[:], ila[:], lag[:, 0:1], None, ALU.add))
            dve.wait_ge(act_c, 1)
            chain(dve.tensor_scalar(a[:], dt[:, :, 0], lr, None, ALU.mult))
            chain(dve.tensor_scalar(b[:], dt[:, :, 1], li, None, ALU.mult))
            for k, src in enumerate((a, b)):
                chain(dve.tensor_scalar(args[:, k, 0, :], src[:], sgn[:, 0:1], None, ALU.mult))
                chain(dve.tensor_scalar(args[:, k, 1, :], args[:, k, 0, :], float(L), None, ALU.mult))
            bb = args[:, 1].rearrange("p k h -> p (k h)")
            tp = 1.0 / (2.0 * np.pi)
            chain(dve.tensor_scalar(turns[:, 0, :], bb, tp, None, ALU.mult))
            chain(dve.tensor_scalar(turns[:, 1, :], turns[:, 0, :], 0.25, None, ALU.add))
            chain(dve.tensor_scalar(turns[:, 2, :], turns[:, 0, :], 0.5, None, ALU.mult))
            chain(dve.tensor_scalar(whole[:], turns[:], ROUND, None, ALU.add))
            chain(dve.tensor_scalar(whole[:], whole[:], ROUND, None, ALU.subtract))
            dve.tensor_tensor(turns[:], turns[:], whole[:], ALU.subtract).then_inc(ready, 1)
            chain(dve.tensor_scalar(f[:], b[:], tp, None, ALU.mult))
            for la in range(LA):
                chain(dve.tensor_scalar(fla[:, 0, la, :], a[:], ila[:, la:la + 1], None, ALU.mult))
                chain(dve.tensor_scalar(tla[:, 0, la, :], f[:], ila[:, la:la + 1], None, ALU.mult))
                chain(dve.tensor_scalar(tla[:, 1, la, :], tla[:, 0, la, :], 0.25, None, ALU.add))
            chain(dve.tensor_scalar(wla[:], tla[:], ROUND, None, ALU.add))
            chain(dve.tensor_scalar(wla[:], wla[:], ROUND, None, ALU.subtract))
            dve.tensor_tensor(wla[:], tla[:], wla[:], ALU.subtract).then_inc(ready, 1)
            dve.wait_ge(act_c, 4)
            chain(dve.scalar_tensor_tensor(t1[:], ex[:], 1.0, th[:], ALU.add, ALU.mult))
            chain(dve.tensor_tensor(t1[:], t1[:], trig[:, 1, :], ALU.mult))
            chain(dve.scalar_tensor_tensor(t2[:], trig[:, 2, :], -2.0, trig[:, 2, :], ALU.mult, ALU.mult))
            chain(dve.tensor_tensor(em[:, 0].rearrange("p k h -> p (k h)"), t1[:], t2[:], ALU.add))
            chain(dve.tensor_tensor(em[:, 1].rearrange("p k h -> p (k h)"), ex[:], trig[:, 0, :], ALU.mult))
            c = lambda i: cc[:, i, :]
            chain(dve.tensor_scalar(c(0), em[:, 1, 1, :], li, None, ALU.mult))
            chain(dve.scalar_tensor_tensor(c(1), em[:, 0, 1, :], lr, c(0), ALU.mult, ALU.subtract))
            chain(dve.tensor_scalar(c(2), em[:, 1, 1, :], lr, None, ALU.mult))
            chain(dve.scalar_tensor_tensor(c(3), em[:, 0, 1, :], li, c(2), ALU.mult, ALU.add))
            chain(dve.tensor_tensor(c(4), c(1), c(1), ALU.mult))
            chain(dve.tensor_tensor(c(5), c(3), c(3), ALU.mult))
            chain(dve.scalar_tensor_tensor(c(4), c(4), 1e-7, c(5), ALU.add, ALU.add))
            chain(dve.reciprocal(c(5), c(4)))
            chain(dve.tensor_tensor(c(1), c(1), c(5), ALU.mult))
            chain(dve.scalar_tensor_tensor(c(3), c(3), -1.0, c(5), ALU.mult, ALU.mult))
            chain(dve.tensor_tensor(c(4), em[:, 0, 0, :], c(1), ALU.mult))
            chain(dve.tensor_tensor(c(5), em[:, 1, 0, :], c(3), ALU.mult))
            chain(dve.tensor_tensor(c(6), c(4), c(5), ALU.subtract))
            chain(dve.tensor_tensor(c(4), em[:, 0, 0, :], c(3), ALU.mult))
            chain(dve.tensor_tensor(c(5), em[:, 1, 0, :], c(1), ALU.mult))
            chain(dve.tensor_tensor(c(7), c(4), c(5), ALU.add))
            dve.wait_ge(act_c, 6)
            chain(dve.tensor_tensor(tla[:, 0], tla[:, 0], ela[:], ALU.mult))
            chain(dve.tensor_tensor(tla[:, 1], tla[:, 1], ela[:], ALU.mult))
            cr = cc[:, 6:7, :].broadcast_to([P, LA, H])
            ci = cc[:, 7:8, :].broadcast_to([P, LA, H])
            chain(dve.tensor_tensor(fla[:, 0], tla[:, 1], cr, ALU.mult))
            chain(dve.tensor_tensor(tA[:], tla[:, 0], ci, ALU.mult))
            chain(dve.tensor_tensor(fla[:, 0], fla[:, 0], tA[:], ALU.subtract))
            chain(dve.tensor_tensor(fla[:, 1], tla[:, 0], cr, ALU.mult))
            chain(dve.tensor_tensor(tA[:], tla[:, 1], ci, ALU.mult))
            chain(dve.tensor_tensor(fla[:, 1], fla[:, 1], tA[:], ALU.add))
            chain(dve.tensor_copy(gg[0:N, 0], fla[0:N, 0]))
            chain(dve.tensor_scalar(gg[N:P, 0], fla[N:P, 1], -1.0, None, ALU.mult))
            chain(dve.tensor_scalar(gg[0:N, 1], fla[0:N, 1], -1.0, None, ALU.mult))
            chain(dve.tensor_scalar(gg[N:P, 1], fla[N:P, 0], -1.0, None, ALU.mult))
            for n in range(2 * B // 4):
                dve.wait_ge(xt_filled, n + 1)
                dst = (wr if n % 2 == 0 else wi)[:, 4 * (n // 2):4 * (n // 2) + 4, :]
                chain(dve.tensor_copy(dst, pt[n % 2][:]))
                dve.sem_inc(xt_read, 1)
            for ch in range(NCH):
                hs = slice(ch * HC, (ch + 1) * HC)
                if ch:
                    dve.wait_ge(sin_ok, ch)
                for j in range(HC):
                    h = ch * HC + j
                    m = dve.tensor_scalar(tt[:, j, :], ilb[:], f[:, h:h + 1], phi[:, 0:1], ALU.mult, ALU.add)
                chain(m)
                chain(dve.tensor_scalar(tw[:], tt[:], ROUND, None, ALU.add))
                chain(dve.tensor_scalar(tw[:], tw[:], ROUND, None, ALU.subtract))
                if ch >= 2:
                    dve.wait_ge(mm_done, (ch - 1) * HC // 2)
                dve.tensor_tensor(tw[:], tt[:], tw[:], ALU.subtract).then_inc(reduced, 1)
                bc = lambda w: w[:, :, hs].rearrange("p c h -> p h c").unsqueeze(2).broadcast_to([P, HC, LA, B])
                bg = lambda k: gg[:, k, :, hs].rearrange("p a h -> p h a").unsqueeze(3).broadcast_to([P, HC, LA, B])
                chain(dve.tensor_tensor(u[:, ch % 2], bc(wr), bg(0), ALU.mult))
                chain(dve.tensor_tensor(u2[:], bc(wi), bg(1), ALU.mult))
                dve.tensor_tensor(u[:, ch % 2], u[:, ch % 2], u2[:], ALU.add).then_inc(u_ok, 1)
                dve.wait_ge(u_ok, ch + 1)

        @block.tensor
        def _(pe):
            pe.wait_ge(twice_ok, 4)
            pe.wait_ge(ident_ok, 1)
            for n in range(2 * B // 4):
                if n >= 2:
                    pe.wait_ge(xt_read, n - 1)
                for k in range(4):
                    cb = 4 * (n // 2) + k
                    m = pe.transpose(pt[n % 2][:, k, :], twice[n % 2][:, cb, :], ident[:])
                m.then_inc(xt_filled, 1)
            for ch in range(NCH):
                pe.wait_ge(u_ok, ch + 1)
                pe.wait_ge(e_ok, ch + 1)
                for j in range(HC):
                    n = (ch * HC + j) // 2
                    if j % 2 == 0 and n >= 4:
                        pe.wait_ge(k_read, n - 3)
                    m = pe.matmul(ps[n % 4][:, j % 2, :], u[:, ch % 2, j].rearrange("p a c -> p (a c)"),
                                  es[:, ch % 2, j, :], start=True, stop=True)
                    if j % 2:
                        m.then_inc(mm_done, 1)


def scale_and_split(nc, ctx, tag, jobs):
    return {k: ctx.enter_context(nc.semaphore(f"{tag}_{k}")) for k in
            ("loaded", "peak", "all_peak", "scale", "hi", "lo", "chain", "made")}


def weight_scales(dve, chain, peak, sc, top):
    chain(dve.tensor_scalar(sc[:, 2:3], peak, 1e-30, None, ALU.max))
    chain(dve.tensor_scalar(sc[:, 3:4].bitcast(I32), sc[:, 2:3].bitcast(I32), 0x7F800000, None, ALU.bitwise_and))
    chain(dve.reciprocal(sc[:, 2:3], sc[:, 3:4]))
    chain(dve.tensor_scalar(sc[:, 0:1], sc[:, 2:3], top, None, ALU.mult))
    chain(dve.tensor_scalar(sc[:, 1:2], sc[:, 3:4], 1.0 / top, None, ALU.mult))


def prep_qkv(nc, wq, wk, wv, qh, ql, kh, kl, qsc, ksc, escale):
    with ExitStack() as ctx:
        sb = lambda n, s, d=F32: ctx.enter_context(nc.sbuf_tensor(n, s, d))
        st = [sb("st_q", [P, KC, QW]), sb("st_k", [P, KC, 2 * KW])]
        peak = sb("peak", [P, 2])
        apeak = sb("apeak", [P, 2])
        s = scale_and_split(nc, ctx, "p2", 2)
        s_k = ctx.enter_context(nc.semaphore("p2_loaded_k"))
        hi, lo, scs, tops = (qh, kh), (ql, kl), (qsc, ksc), (TOP["q"], TOP["k"])
        block = ctx.enter_context(nc.Block())

        @block.sync
        def _(sp):
            sp.dma_start(st[0][:], wq.rearrange("(k p) n -> p k n", p=P)).then_inc(s["loaded"], 16)
            sp.dma_start(st[1][:, :, 0:KW], wk.rearrange("(k p) n -> p k n", p=P)).then_inc(s_k, 16)
            sp.dma_start(st[1][:, :, KW:2 * KW], wv.rearrange("(k p) n -> p k n", p=P)).then_inc(s_k, 16)

        @block.gpsimd
        def _(pool):
            for n in range(2):
                pool.wait_ge(s["peak"], n + 1)
                pool.partition_all_reduce(apeak[:, n:n + 1], peak[:, n:n + 1], P, RMAX).then_inc(s["all_peak"], 1)

        @block.scalar
        def _(act):
            for n in range(2):
                act.wait_ge(s["scale"], n + 1)
                for k in range(KC):
                    act.activation(hi[n][:, k], st[n][:, k], ACT.Copy, scale=scs[n][:, 0:1]).then_inc(s["hi"], 1)

        @block.vector
        def _(dve):
            chain = Chain(dve, s["chain"])
            dve.wait_ge(s["loaded"], 16)
            dve.tensor_reduce(peak[:, 0:1], st[0][:].rearrange("p k n -> p (k n)"), AX.X, ALU.max,
                              apply_absolute_value=True).then_inc(s["peak"], 1)
            dve.wait_ge(s_k, 32)
            dve.tensor_reduce(peak[:, 1:2], st[1][:].rearrange("p k n -> p (k n)"), AX.X, ALU.max,
                              apply_absolute_value=True).then_inc(s["peak"], 1)
            for n in range(2):
                dve.wait_ge(s["all_peak"], n + 1)
                weight_scales(dve, chain, apeak[:, n:n + 1], scs[n], tops[n])
                dve.sem_inc(s["scale"], 1)
            chain(dve.scalar_tensor_tensor(escale[:], qsc[:, 1:2], float(HD) ** -0.5, ksc[:, 1:2], ALU.mult, ALU.mult))
            for n in range(2):
                for k in range(KC):
                    dve.wait_ge(s["hi"], n * KC + k + 1)
                    dve.scalar_tensor_tensor(lo[n][:, k], st[n][:, k], scs[n][:, 0:1], hi[n][:, k],
                                             ALU.mult, ALU.subtract)


def attention(nc, hcat, acat, qh, ql, kh, kl, escale):
    T = (P, TXT)
    with ExitStack() as ctx:
        sb = lambda n, s, d=F32: ctx.enter_context(nc.sbuf_tensor(n, s, d))
        sem = lambda n: ctx.enter_context(nc.semaphore(n))
        ident = sb("ident3", [P, P])
        ident_bf = sb("ident_bf", [P, P], BF16)
        mask = sb("mask", [P, REP, P], BF16)
        xin = sb("xin", [P, 2, D])
        xth, xtl = sb("xth", [P, KC, S], F16), sb("xtl", [P, KC, S], F16)
        qsh, qsl = sb("qsh", [P, KC, S], F16), sb("qsl", [P, KC, S], F16)
        ksh, ksl = sb("ksh", [P, 2, S], F16), sb("ksl", [P, 2, S], F16)
        vsh, vsl = sb("vsh", [P, 2, NKV, HD + 1], F16), sb("vsl", [P, 2, NKV, HD + 1], F16)
        mh, ml = sb("mh", [NH, S], F16), sb("ml", [NH, S], F16)
        qst = [sb(f"qst{i}", [STACK + 2, NH, S], F16) for i in range(2)]
        kst = [sb(f"kst{i}", [STACK + 2, NKV, S], F16) for i in range(2)]
        vh = [sb(f"vh{i}", [P, 2, NKV, HD + 1], F16) for i in range(2)]
        vl = [sb(f"vl{i}", [P, 2, NKV, HD + 1], F16) for i in range(2)]
        p32 = sb("p32", [P, 2, 3, 2 * S])
        ph = sb("ph", [P, 2, 3, 2 * S], F16)
        pl = sb("pl", [P, 2, 3, 2 * S], F16)
        mx = sb("mx", [P, 2, NH])
        rden = sb("rden", [P, 2, REP])
        ao = sb("ao", [P, 2, 2, D])
        stats = sb("stats", [P, 2, 2, 6])
        mv = sb("mv", [P, 2, 2])
        rs = sb("rs", [P, 4, 2])
        psS = [ctx.enter_context(nc.psum_tensor(f"psS{i}", [P, 512], F32)) for i in range(2)]
        psT = [ctx.enter_context(nc.psum_tensor(f"psT{i}", [P, 512], F32)) for i in range(2)]
        psO = [ctx.enter_context(nc.psum_tensor(f"psO{i}", [P, 2, REP, HD + 1], F32)) for i in range(2)]
        psJ = [ctx.enter_context(nc.psum_tensor(f"psJ{i}", [P, 512], F32)) for i in range(2)]
        passed = sem("passed3")
        pool_c, dve_c, dve_ln, const_ok = sem("pool_c3"), sem("dve_c3"), sem("dve_ln"), sem("const_ok")
        x_in, ln_done = sem("x_in"), sem("ln_done")
        pj_filled, pj_hi, pj_lo = sem("pj_filled"), sem("pj_hi"), sem("pj_lo")
        s_filled, s_read = sem("s_filled"), sem("s_read")
        st_filled, exp_done, masked, hi_done, lo_done = (sem("st_filled"), sem("exp_done"), sem("masked"),
                                                         sem("hi_done"), sem("lo_done"))
        av_done, norm_done, rec_done = sem("av_done"), sem("norm_done"), sem("rec_done")
        q_in = [sem(f"q_in{c}") for c in range(KC)]
        k_in = [sem(f"k_in{c}") for c in range(2)]
        m_in, v_in = sem("m_in"), sem("v_in")
        a_out = [sem("a_out0"), sem("a_out1")]

        SLOTS = range(NKV)
        MAXES = [[0, 1]] + [[s + 1] for s in range(1, NKV - 1)] + [[]]
        EXTRA = {2: ("v", 0), 3: ("v", 1), 4: ("k", 0), 5: ("k", 1)}

        def units(has):
            out = []
            for s in SLOTS:
                row = []
                if s == NKV - 1 and has["max"]:
                    row.append(("m", 0))
                if has["qkv"]:
                    row.append(("q", s))
                    if s in EXTRA:
                        row.append(EXTRA[s])
                if s == NKV - 1 and has["ln"]:
                    row += [("x", n) for n in range(4)]
                out.append(row)
            return out

        def parts(b):
            return {"att": b >= 0, "max": 0 <= b + 1 < B, "qkv": 0 <= b + 2 < B, "ln": 0 <= b + 3 < B}

        def count(b):
            return sum(map(len, units(parts(b))))

        FULL = parts(0)
        PER = count(0)
        BEFORE = {b: sum(count(c) for c in range(-3, b)) for b in range(-3, B + 1)}

        def before(b, par):
            return BEFORE[b] if isinstance(b, int) else BEFORE[2] - 2 * PER + b * PER

        def odd(b, par):
            return (BEFORE[b] if isinstance(b, int) else BEFORE[2 + par]) % 2

        def at(rows, kind, n=0):
            return sum(rows, []).index((kind, n))

        def steps(eng, step):
            for b in range(-3, 2):
                step(b, b % 2, parts(b))
            with eng.Fori(1, 14) as i:
                step(i * 2, 0, FULL)
                step(i * 2 + 1, 1, FULL)
            for b in range(28, B):
                step(b, b % 2, parts(b))

        def view(t, slot, k):
            if k < 2:
                return t[:, slot, k, :].rearrange("p (h i) -> p h i", i=S)
            return t[0:TXT, slot, k, 0:REP * TXT].rearrange("p (h i) -> p h i", i=TXT)

        def ps_view(t, k):
            if k < 2:
                return t[:, 0:2 * S].rearrange("p (h i) -> p h i", i=S)
            return t[0:TXT, 0:REP * TXT].rearrange("p (h i) -> p h i", i=TXT)

        def unit_views(kind, n, bank):
            ps = psJ[bank]
            if kind == "q":
                return ps[:, 0:S], qsh[:, n, :], qsl[:, n, :]
            if kind == "k":
                return ps[:, 0:S], ksh[:, n, :], ksl[:, n, :]
            if kind == "v":
                r = T[n]
                return (ps[0:r, 0:KW].rearrange("p (g d) -> p g d", d=HD), vsh[0:r, n, :, 0:HD],
                        vsl[0:r, n, :, 0:HD])
            if kind == "m":
                return ps[0:NH, 0:S], mh[:], ml[:]
            t, half = divmod(n, 2)
            cols = slice(t * P, t * P + T[t])
            return (ps[:, 0:4 * T[t]].rearrange("p (c j) -> p c j", j=T[t]),
                    xth[:, 4 * half:4 * half + 4, cols], xtl[:, 4 * half:4 * half + 4, cols])

        def free_place(eng, kind, n, b):
            if kind == "q":
                wait(eng, q_in[n], 16 * 12 * (b + 2))
            if kind == "k":
                wait(eng, k_in[n], 16 * 12 * (b + 2))
            if kind == "v":
                wait(eng, v_in, 32 * (b + 2))
            if kind == "m":
                wait(eng, m_in, 32 * (b + 1))

        block = ctx.enter_context(nc.Block())

        @block.sync
        def _(sp):
            def restack(src_hi, src_lo, dst, c, heads, arrived):
                for k, src in enumerate((src_hi, src_hi, src_lo) if heads is not None and dst[1] == "q" else
                                        (src_hi, src_lo, src_hi)):
                    for r in range(4):
                        sp.dma_start(dst[0][k * HD:(k + 1) * HD, 4 * c + r, :],
                                     src[r * HD:(r + 1) * HD, c, :]).then_inc(arrived, 16)

            def step(b, par, has):
                base = before(b, par)
                rows = units(has)
                early = isinstance(b, int)
                nxt = 1 - par
                if has["max"]:
                    wait(sp, st_filled, 24 * b)
                    pass_on(sp, passed)
                    prev = parts(b - 1) if early else FULL
                    wait(sp, pj_lo, before(b - 1, nxt) + at(units(prev), "q", NKV - 1) + 1)
                    restack(qsh, qsl, (qst[nxt], "q"), 7, 1, q_in[7])
                    restack(ksh, ksl, (kst[nxt], "k"), 1, 1, k_in[1])
                    wait(sp, av_done, 8 * b)
                    pass_on(sp, passed)
                    sp.dma_start(vh[nxt][:], vsh[:]).then_inc(v_in, 16)
                    sp.dma_start(vl[nxt][:], vsl[:]).then_inc(v_in, 16)
                if has["ln"]:
                    wait(sp, pj_filled, base)
                    pass_on(sp, passed)
                    sp.dma_start(xin[:, 0, :], hcat[bass.ds((b + 3) * S, P), :]).then_inc(x_in, 16)
                    sp.dma_start(xin[0:TXT, 1, :], hcat[bass.ds((b + 3) * S + P, TXT), :]).then_inc(x_in, 16)
                if not early or b >= 1:
                    store(b - 1, nxt)
                for s in range(NKV - 1):
                    if has["qkv"]:
                        wait(sp, pj_lo, base + at(rows, "q", s) + 1)
                        pass_on(sp, passed)
                        wait(sp, st_filled, 24 * b + 3 * (s + 1))
                        restack(qsh, qsl, (qst[par], "q"), s, 1, q_in[s])
                        if s == 4:
                            wait(sp, pj_lo, base + at(rows, "k", 0) + 1)
                            restack(ksh, ksl, (kst[par], "k"), 0, 1, k_in[0])
                if has["max"]:
                    wait(sp, pj_lo, base + at(rows, "m") + 1)
                    sp.dma_start(qst[nxt][STACK:STACK + 1, :, :], mh[:]).then_inc(m_in, 16)
                    sp.dma_start(qst[nxt][STACK + 1:STACK + 2, :, :], ml[:]).then_inc(m_in, 16)

            def store(b, par):
                sp.wait_ge(norm_done, 8 * b + 8)
                pass_on(sp, passed)
                sp.dma_start(acat[bass.ds(b * S, P), :], ao[:, par, 0, :]).then_inc(a_out[par], 16)
                sp.dma_start(acat[bass.ds(b * S + P, TXT), :], ao[0:TXT, par, 1, :]).then_inc(a_out[par], 16)

            sp.wait_ge(const_ok, 1)
            steps(sp, step)
            store(B - 1, (B - 1) % 2)
            for q in a_out:
                sp.wait_ge(q, 32 * B // 2)

        @block.gpsimd
        def _(pool):
            chain = Chain(pool, pool_c)
            chain(pool.memset(ident[:], 0.0))
            chain(pool.affine_select(out=ident[:], in_=ident[:], compare_op=ALU.not_equal, fill=1.0, base=0,
                                     pattern=[[-1, P]], channel_multiplier=1))
            chain(pool.tensor_copy(ident_bf[:], ident[:]))
            chain(pool.memset(mask[:], 0.0))
            chain(pool.affine_select(out=mask[:], in_=mask[:], compare_op=ALU.is_ge, fill=-1e38, base=0,
                                     pattern=[[0, REP], [-1, P]], channel_multiplier=1))
            for i in range(2):
                chain(pool.memset(kst[i][STACK:STACK + 2], MROW))
            chain(pool.memset(vsh[:], 0.0))
            chain(pool.memset(vsl[:], 0.0))
            chain(pool.memset(vsh[:, :, :, HD:HD + 1], 1.0))
            chain(pool.memset(mv[:], 1.0))
            chain(pool.memset(p32[:, :, 2, :], 0.0))
            pool.memset(xin[:, 1, :], 0.0).then_inc(const_ok, 1)

            def step(b, par, has):
                if not has["att"]:
                    return
                for g in SLOTS:
                    for k in range(3):
                        pool.wait_ge(exp_done, 24 * b + 3 * g + k + 1)
                        pass_on(pool, passed)
                        v = view(p32, g % 2, k)
                        v = v[:, :, 0:P] if k < 2 else v
                        w = v.shape[2]
                        pool.affine_select(out=v, in_=v, compare_op=ALU.is_ge, fill=0.0, base=0,
                                           pattern=[[0, v.shape[1]], [1, w]],
                                           channel_multiplier=-1).then_inc(masked, 1)

            steps(pool, step)

        @block.scalar
        def _(act):
            act.wait_ge(const_ok, 1)

            def step(b, par, has):
                base, k0 = before(b, par), odd(b, par)
                rows = units(has)
                n = 0
                for g in SLOTS:
                    if has["att"]:
                        for k in range(3):
                            act.wait_ge(st_filled, 24 * b + 3 * g + k + 1)
                            wait(act, lo_done, 24 * b + 3 * (g - 2) + k + 1)
                            act.activation(view(p32, g % 2, k), ps_view(psT[(g + k) % 2], k), ACT.Exp,
                                           scale=(escale[:, 0:1] if k < 2 else escale[0:TXT, 0:1])
                                           ).then_inc(exp_done, 1)
                        wait(act, av_done, 8 * b + g - 1)
                        for k in range(3):
                            act.wait_ge(masked, 24 * b + 3 * g + k + 1)
                            act.copy(view(ph, g % 2, k), view(p32, g % 2, k)).then_inc(hi_done, 1)
                    for kind, m in rows[g]:
                        src, hi, _ = unit_views(kind, m, (k0 + n) % 2)
                        act.wait_ge(pj_filled, base + n + 1)
                        free_place(act, kind, m, b)
                        if kind == "m":
                            act.mul(hi, src, -1.0 / MROW).then_inc(pj_hi, 1)
                        else:
                            act.copy(hi, src).then_inc(pj_hi, 1)
                        n += 1

            steps(act, step)

        @block.vector
        def _(dve):
            dve.wait_ge(const_ok, 1)

            def norm(b, par, g):
                n = 8 * b + g
                if g == 0:
                    wait(dve, a_out[par], 16 * (b - par))
                dve.wait_ge(av_done, n + 1)
                o = psO[g % 2]
                dve.reciprocal(rden[:, 0, :], o[:, 0, :, HD]).then_inc(rec_done, 1)
                dve.reciprocal(rden[0:TXT, 1, :], o[0:TXT, 1, :, HD]).then_inc(rec_done, 1)
                dve.wait_ge(rec_done, 2 * n + 2)
                for t in range(2):
                    r = T[t]
                    dst = ao[0:r, par, t, g * P:(g + 1) * P].rearrange("p (h d) -> p h d", d=HD)
                    ins = dve.tensor_tensor(dst, o[0:r, t, :, 0:HD],
                                            rden[0:r, t, :].unsqueeze(2).broadcast_to([r, REP, HD]), ALU.mult)
                ins.then_inc(norm_done, 1)

            def layer_norm(b):
                LINKS = 20
                chain = Chain(dve, dve_ln)
                chain.base = LINKS * (b + 3)
                dve.wait_ge(x_in, 32 * (b + 4))
                for t in range(2):
                    for h in range(2):
                        chain(dve.bn_stats(stats[0:T[t], t, h, :], xin[0:T[t], t, 512 * h:512 * h + 512]), passed)
                    chain(dve.bn_aggr(mv[0:T[t], t, :], stats[0:T[t], t]))
                rsqrt(dve, chain, rs, mv[:, :, 1])
                for t in range(2):
                    r = T[t]
                    ins = dve.tensor_scalar(xin[0:r, t, :], xin[0:r, t, :], mv[0:r, t, 0:1],
                                            rs[0:r, 3, t:t + 1], ALU.subtract, ALU.mult)
                    if t == 0:
                        chain(ins)
                    else:
                        ins.then_inc(ln_done, 1)
                        chain.n += 1
                        dve.sem_inc(dve_ln, 1)
                assert chain.n == LINKS, chain.n
                dve.wait_ge(ln_done, b + 4)

            def step(b, par, has):
                base, k0 = before(b, par), odd(b, par)
                rows = units(has)
                n = 0
                for g in SLOTS:
                    if has["att"] and g:
                        norm(b, par, g - 1)
                    if has["max"]:
                        for j in MAXES[g]:
                            for k in range(3):
                                u = 24 * (b + 1) + 3 * j + k
                                dve.wait_ge(s_filled, u + 1)
                                if j == 0 and k == 0:
                                    wait(dve, pj_filled, base)
                                src = psS[(j + k) % 2]
                                if k == 0:
                                    v, dst = src[:].rearrange("p (h i) -> p h i", i=P), mx[:, 0, 4 * j:4 * j + 4]
                                else:
                                    v = src[0:TXT, 0:2 * S].rearrange("p (h i) -> p h i", i=S)
                                    dst = mx[0:TXT, 1, 4 * j + 2 * k - 2:4 * j + 2 * k]
                                dve.tensor_reduce(dst, v, AX.X, ALU.max).then_inc(s_read, 1)
                    if has["att"]:
                        for k in range(3):
                            dve.wait_ge(hi_done, 24 * b + 3 * g + k + 1)
                            dve.tensor_tensor(view(pl, g % 2, k), view(p32, g % 2, k), view(ph, g % 2, k),
                                              ALU.subtract).then_inc(lo_done, 1)
                    for kind, m in rows[g]:
                        src, hi, lo = unit_views(kind, m, (k0 + n) % 2)
                        dve.wait_ge(pj_hi, base + n + 1)
                        if kind == "m":
                            dve.scalar_tensor_tensor(lo, src, -1.0 / MROW, hi, ALU.mult,
                                                     ALU.subtract).then_inc(pj_lo, 1)
                        else:
                            dve.tensor_tensor(lo, src, hi, ALU.subtract).then_inc(pj_lo, 1)
                        n += 1
                    if has["ln"] and g == 3:
                        layer_norm(b)
                if has["att"]:
                    norm(b, par, NKV - 1)

            steps(dve, step)

        @block.tensor
        def _(pe):
            pe.wait_ge(const_ok, 1)

            def scores(b, par, g):
                if g == 0:
                    pe.wait_ge(m_in, 32 * (b + 1))
                K, Q = kst[par], qst[par]
                for k in range(3):
                    u = 24 * b + 3 * g + k
                    wait(pe, exp_done, u - 1)
                    ps = psT[(g + k) % 2]
                    if k < 2:
                        m = pe.matmul(ps[:, 0:2 * S], K[:, g, 0:P], Q[:, 4 * g + 2 * k:4 * g + 2 * k + 2, :],
                                      start=True, stop=True)
                    else:
                        m = pe.matmul(ps[0:TXT, 0:REP * TXT], K[:, g, P:S], Q[:, 4 * g:4 * g + 4, P:S],
                                      start=True, stop=True)
                    m.then_inc(st_filled, 1)

            def weigh(b, par, g):
                if g == 0:
                    pe.wait_ge(v_in, 32 * (b + 1))
                pe.wait_ge(lo_done, 24 * b + 3 * g + 3)
                wait(pe, norm_done, 8 * b + g - 1)
                o = psO[g % 2]
                VH, VL = vh[par], vl[par]
                for r in range(REP):
                    def blocks(t):
                        v = view(t, g % 2, r // 2)[:, r % 2, :]
                        return v[:, 0:P], v[:, P:S], view(t, g % 2, 2)[:, r, :]
                    (h00, h01, h11), (l00, l01, l11) = blocks(ph), blocks(pl)
                    first = [(h00, VH, 0), (h00, VL, 0), (l00, VH, 0)]
                    second = [(h01, VH, 0), (h01, VL, 0), (l01, VH, 0), (h11, VH, 1), (h11, VL, 1), (l11, VH, 1)]
                    for t, list_ in enumerate((first, second)):
                        for n, (p, v, j) in enumerate(list_):
                            m = pe.matmul(o[0:T[t], t, r, :], p, v[0:T[j], j, g, :],
                                          start=n == 0, stop=n == len(list_) - 1)
                m.then_inc(av_done, 1)

            def score_rows(b, par, j):
                pe.wait_ge(q_in[j], 16 * 12 * (b + 1))
                pe.wait_ge(k_in[j // 4], 16 * 12 * (b + 1))
                K, Q = kst[par], qst[par]
                for k in range(3):
                    u = 24 * b + 3 * j + k
                    wait(pe, s_read, u - 1)
                    ps = psS[(j + k) % 2]
                    if k == 0:
                        pe.matmul(ps[:], ident_bf[:], mask[:], start=True, stop=False, skip_group_check=True)
                        for r in range(REP):
                            m = pe.matmul(ps[:, r * P:(r + 1) * P], Q[0:STACK, 4 * j + r, 0:P], K[0:STACK, j, 0:P],
                                          start=False, stop=r == REP - 1, skip_group_check=True)
                    else:
                        v = ps[0:TXT, 0:2 * S].rearrange("p (h i) -> p h i", i=S)
                        pe.matmul(v[:, :, P:S], ident_bf[0:TXT, 0:TXT], mask[0:TXT, 0:2, 0:TXT],
                                  start=True, stop=False, skip_group_check=True)
                        for r in range(2):
                            m = pe.matmul(v[:, r, :], Q[0:STACK, 4 * j + 2 * (k - 1) + r, P:S], K[0:STACK, j, :],
                                          start=False, stop=r == 1, skip_group_check=True)
                    m.then_inc(s_filled, 1)

            def unit(kind, n, bank, b):
                ps = psJ[bank]
                if kind in "qk":
                    wh, wl = (qh, ql) if kind == "q" else (kh, kl)
                    c = slice(n * P, (n + 1) * P)
                    for k in range(KC):
                        pe.matmul(ps[:, 0:S], wh[:, k, c], xth[:, k, :], start=k == 0, stop=False)
                        pe.matmul(ps[:, 0:S], wh[:, k, c], xtl[:, k, :], start=False, stop=False)
                        m = pe.matmul(ps[:, 0:S], wl[:, k, c], xth[:, k, :], start=False, stop=k == KC - 1)
                elif kind == "v":
                    r, c = T[n], slice(n * P, n * P + T[n])
                    for k in range(KC):
                        pe.matmul(ps[0:r, 0:KW], xth[:, k, c], kh[:, k, KW:], start=k == 0, stop=False)
                        pe.matmul(ps[0:r, 0:KW], xth[:, k, c], kl[:, k, KW:], start=False, stop=False)
                        m = pe.matmul(ps[0:r, 0:KW], xtl[:, k, c], kh[:, k, KW:], start=False, stop=k == KC - 1)
                elif kind == "m":
                    pe.wait_ge(s_read, 24 * (b + 2))
                    pe.transpose(ps[0:NH, 0:P], mx[:, 0, :], ident[:])
                    m = pe.transpose(ps[0:NH, P:S], mx[0:TXT, 1, :], ident[0:TXT, 0:TXT])
                else:
                    t, half = divmod(n, 2)
                    pe.wait_ge(ln_done, b + 4)
                    r = T[t]
                    for k in range(4):
                        c = 4 * half + k
                        m = pe.transpose(ps[:, k * r:(k + 1) * r], xin[0:r, t, c * P:(c + 1) * P], ident[0:r, 0:r])
                m.then_inc(pj_filled, 1)

            def step(b, par, has):
                base, k0 = before(b, par), odd(b, par)
                rows = units(has)
                n = 0
                for g in SLOTS:
                    if has["att"]:
                        scores(b, par, g)
                        if g:
                            weigh(b, par, g - 1)
                    if has["max"]:
                        for j in MAXES[g]:
                            score_rows(b + 1, 1 - par, j)
                    for kind, m in rows[g]:
                        wait(pe, pj_lo, base + n if n == 0 else base + n - 1)
                        unit(kind, m, (k0 + n) % 2, b)
                        n += 1
                if has["att"]:
                    weigh(b, par, NKV - 1)

            steps(pe, step)


def rsqrt(dve, chain, rs, var):
    v, y, t, out = (rs[:, k, :] for k in range(4))
    chain(dve.tensor_scalar(v, var, EPS_LN, None, ALU.add))
    chain(dve.tensor_scalar(t.bitcast(I32), v.bitcast(I32), 1, None, ALU.logical_shift_right))
    chain(dve.tensor_scalar(y.bitcast(I32), t.bitcast(I32), -1.0, float(0x5F3759DF), ALU.mult, ALU.add))
    for n in range(3):
        chain(dve.tensor_tensor(t, y, y, ALU.mult))
        chain(dve.scalar_tensor_tensor(t, t, -0.5, v, ALU.mult, ALU.mult))
        chain(dve.scalar_tensor_tensor(out if n == 2 else y, t, 1.5, y, ALU.add, ALU.mult))


def prep_out(nc, wo, w_base, enc0, enc1, coefs, masks, fourier, woh, wol, wfh, wfl, osc, fsc, ksc):
    HALF = 512
    with ExitStack() as ctx:
        sb = lambda n, s, d=F32: ctx.enter_context(nc.sbuf_tensor(n, s, d))
        sem = lambda n: ctx.enter_context(nc.semaphore(n))
        st = [sb("st_o", [P, KC, D]), sb("st_f", [P, KC, D])]
        wb = sb("wb", [P, KC, D])
        fm = sb("fm", [P, 2, D])
        ident = sb("ident4", [P, P])
        enc = sb("enc", [R, D])
        cf = [sb("cf0", [P, KC, E, R0]), sb("cf1", [P, KC, E, R1])]
        mk = [sb("mk0", [P, KC, E, R0], I32), sb("mk1", [P, KC, E, R1], I32)]
        mf = [sb("mf0", [P, KC, E, R0]), sb("mf1", [P, KC, E, R1])]
        cm = sb("cm", [P, KC, R])
        gt = sb("gt", [R, D])
        peak, apeak = sb("peak4", [P, 2]), sb("apeak4", [P, 2])
        psG = [ctx.enter_context(nc.psum_tensor(f"psG{i}", [P, HALF], F32)) for i in range(2)]
        psW = [ctx.enter_context(nc.psum_tensor(f"psW{i}", [P, HALF], F32)) for i in range(4)]
        s = scale_and_split(nc, ctx, "p4", 2)
        in_c, in_b, in_e = sem("in_c"), sem("in_b"), sem("in_e")
        in_f = [sem("in_f0"), sem("in_f1")]
        cm_ok, id_ok, pool_c, f_used, g_done, g_ok, w_filled, w_read = (sem(n) for n in (
            "cm_ok", "id_ok", "pool_c4", "f_used", "g_done", "g_ok", "w_filled", "w_read"))
        hi, lo, scs, tops = (woh, wfh), (wol, wfl), (osc, fsc), (TOP["o"], TOP["f"])
        block = ctx.enter_context(nc.Block())

        @block.sync
        def _(sp):
            for n in range(2):
                sp.dma_start(cf[n][:].rearrange("p k e r -> p k e r"),
                             coefs[n].rearrange("e (k p) r -> p k e r", p=P)) if False else None
                for e in range(E):
                    sp.dma_start(cf[n][:, :, e, :], coefs[n][e].rearrange("(k p) r -> p k r", p=P)).then_inc(in_c, 16)
                    sp.dma_start(mk[n][:, :, e, :], masks[n][e].rearrange("(k p) r -> p k r", p=P)).then_inc(in_c, 16)
            sp.dma_start(enc[0:R0, :], enc0).then_inc(in_e, 16)
            sp.dma_start(enc[R0:R, :], enc1).then_inc(in_e, 16)
            sp.dma_start(wb[:], w_base.rearrange("(k p) n -> p k n", p=P)).then_inc(in_b, 16)
            for k in range(KC):
                if k >= 2:
                    sp.wait_ge(f_used, k - 1)
                sp.dma_start(fm[:, k % 2, :], fourier[k * P:(k + 1) * P, :]).then_inc(in_f[k % 2], 16)
            sp.dma_start(st[0][:], wo.rearrange("(k p) n -> p k n", p=P)).then_inc(s["loaded"], 16)

        @block.gpsimd
        def _(pool):
            chain = Chain(pool, pool_c)
            chain(pool.memset(ident[:], 0.0))
            pool.affine_select(out=ident[:], in_=ident[:], compare_op=ALU.not_equal, fill=1.0, base=0,
                               pattern=[[-1, P]], channel_multiplier=1).then_inc(id_ok, 1)
            for n in range(2):
                pool.wait_ge(s["peak"], n + 1)
                pool.partition_all_reduce(apeak[:, n:n + 1], peak[:, n:n + 1], P, RMAX).then_inc(s["all_peak"], 1)

        @block.tensor
        def _(pe):
            pe.wait_ge(cm_ok, 1)
            for k in range(KC):
                pe.wait_ge(in_f[k % 2], 16 * (k // 2 + 1))
                for h in range(2):
                    m = pe.matmul(psG[h][0:R, :], cm[:, k, :], fm[:, k % 2, h * HALF:(h + 1) * HALF],
                                  start=k == 0, stop=k == KC - 1)
                m.then_inc(f_used, 1)
            pe.wait_ge(g_ok, 1)
            pe.wait_ge(in_e, 32)
            pe.wait_ge(in_b, 16)
            pe.wait_ge(id_ok, 1)
            for n in range(2 * KC):
                k, h = divmod(n, 2)
                if n >= 4:
                    pe.wait_ge(w_read, n - 3)
                c = slice(k * P, (k + 1) * P)
                for j in range(4):
                    pe.matmul(psW[n % 4][:, j * P:(j + 1) * P], wb[:, 4 * h + j, c], ident[:],
                              start=j == 0, stop=False, skip_group_check=True)
                m = pe.matmul(psW[n % 4][:], enc[:, c], gt[:, h * HALF:(h + 1) * HALF], start=False, stop=True,
                              skip_group_check=True)
                m.then_inc(w_filled, 1)

        @block.scalar
        def _(act):
            for n in range(2 * KC):
                k, h = divmod(n, 2)
                act.wait_ge(w_filled, n + 1)
                act.copy(st[1][:, k, h * HALF:(h + 1) * HALF], psW[n % 4][:]).then_inc(w_read, 1)
            for n in range(2):
                act.wait_ge(s["scale"], n + 1)
                for k in range(KC):
                    act.activation(hi[n][:, k], st[n][:, k], ACT.Copy, scale=scs[n][:, 0:1]).then_inc(s["hi"], 1)

        @block.vector
        def _(dve):
            chain = Chain(dve, s["chain"])
            dve.wait_ge(in_c, 16 * 4 * E)
            for n, (lo_r, hi_r) in enumerate(((0, R0), (R0, R))):
                chain(dve.tensor_copy(mf[n][:], mk[n][:]))
                chain(dve.tensor_tensor(cf[n][:], cf[n][:], mf[n][:], ALU.mult))
                chain(dve.tensor_tensor(mf[n][:, :, 0, :], cf[n][:, :, 0, :], cf[n][:, :, 1, :], ALU.add))
                chain(dve.tensor_tensor(cm[:, :, lo_r:hi_r], mf[n][:, :, 0, :], cf[n][:, :, 2, :], ALU.add))
            dve.sem_inc(cm_ok, 1)
            dve.wait_ge(f_used, KC)
            for h in range(2):
                m = dve.tensor_scalar(gt[:, h * HALF:(h + 1) * HALF], psG[h][0:R, :], 0.5, None, ALU.mult)
            m.then_inc(g_ok, 1)
            dve.wait_ge(s["loaded"], 16)
            dve.tensor_reduce(peak[:, 0:1], st[0][:].rearrange("p k n -> p (k n)"), AX.X, ALU.max,
                              apply_absolute_value=True).then_inc(s["peak"], 1)
            dve.wait_ge(w_read, 2 * KC)
            dve.tensor_reduce(peak[:, 1:2], st[1][:].rearrange("p k n -> p (k n)"), AX.X, ALU.max,
                              apply_absolute_value=True).then_inc(s["peak"], 1)
            for n in range(2):
                dve.wait_ge(s["all_peak"], n + 1)
                weight_scales(dve, chain, apeak[:, n:n + 1], scs[n], tops[n])
                dve.sem_inc(s["scale"], 1)
            chain(dve.tensor_tensor(osc[:, 2:3], osc[:, 1:2], ksc[:, 1:2], ALU.mult))
            for n in range(2):
                for k in range(KC):
                    dve.wait_ge(s["hi"], n * KC + k + 1)
                    dve.scalar_tensor_tensor(lo[n][:, k], st[n][:, k], scs[n][:, 0:1], hi[n][:, k],
                                             ALU.mult, ALU.subtract)


def output(nc, hcat, acat, bias, out, woh, wol, wfh, wfl, osc, fsc):
    HALF = 512
    NT = -(-ROWS // P)
    LAST = ROWS - P
    NEW = ROWS - (NT - 1) * P
    with ExitStack() as ctx:
        sb = lambda n, s, d=F32: ctx.enter_context(nc.sbuf_tensor(n, s, d))
        sem = lambda n: ctx.enter_context(nc.semaphore(n))
        ident = sb("ident5", [P, P])
        bias_sb = sb("bias_sb", [P, D])
        a_in = sb("a_in", [P, 2, D])
        h_in = sb("h_in", [P, 2, D])
        h2 = sb("h2", [P, D])
        hb = sb("hb", [P, 2, D])
        xh = sb("xh", [P, D])
        y = sb("y", [P, 2, D])
        ath, atl = sb("ath", [P, KC, P], F16), sb("atl", [P, KC, P], F16)
        xth, xtl = sb("xth5", [P, KC, P], F16), sb("xtl5", [P, KC, P], F16)
        stats, mv, rs = sb("stats5", [P, 2, 6]), sb("mv5", [P, 2]), sb("rs5", [P, 4, 1])
        psT = [ctx.enter_context(nc.psum_tensor(f"ps5T{i}", [P, HALF], F32)) for i in range(4)]
        psO = [ctx.enter_context(nc.psum_tensor(f"ps5O{i}", [P, HALF], F32)) for i in range(2)]
        psF = [ctx.enter_context(nc.psum_tensor(f"ps5F{i}", [P, HALF], F32)) for i in range(2)]
        passed = sem("passed5")
        pool_c, const_ok, bias_in = sem("pool_c5"), sem("const_ok5"), sem("bias_in")
        a_arr = [sem("a_arr0"), sem("a_arr1")]
        h_arr = [sem("h_arr0"), sem("h_arr1")]
        out_ok = [sem("out_ok0"), sem("out_ok1")]
        a_filled, a_hi, a_lo = sem("a_filled"), sem("a_hi"), sem("a_lo")
        x_filled, x_hi, x_lo = sem("x_filled"), sem("x_hi"), sem("x_lo")
        o_filled, o_read, f_filled, f_read = sem("o_filled"), sem("o_read"), sem("f_filled"), sem("f_read")
        ln_c, ln_done, hb_done = sem("ln_c"), sem("ln_done5"), sem("hb_done")

        def parts(t):
            return {"o": 0 <= t < NT, "a": 0 <= t + 1 < NT, "f": 0 <= t - 1 < NT}

        def steps(eng, step):
            for t in range(-1, 2):
                step(t, t % 2, parts(t))
            with eng.Fori(1, NT // 2 - 2) as i:
                step(i * 2, 0, parts(2))
                step(i * 2 + 1, 1, parts(3))
            for t in range(NT - 4, NT + 1):
                step(t, t % 2, parts(t))

        def row(t):
            return LAST if isinstance(t, int) and t == NT - 1 else t * P

        block = ctx.enter_context(nc.Block())

        @block.sync
        def _(sp):
            sp.dma_start(bias_sb[:], bias.rearrange("(o d) -> o d", o=1).broadcast_to([P, D])).then_inc(bias_in, 16)

            def load_a(t, par):
                wait(sp, a_filled, 2 * (t - 1))
                pass_on(sp, passed)
                sp.dma_start(a_in[:, par, :], acat[bass.ds(row(t), P), :]).then_inc(a_arr[par], 16)

            def load_h(t, par):
                wait(sp, o_read, 2 * (t - 1))
                pass_on(sp, passed)
                sp.dma_start(h_in[:, par, :], hcat[bass.ds(row(t), P), :]).then_inc(h_arr[par], 16)

            def store(t, par):
                sp.wait_ge(f_read, 2 * t + 2)
                pass_on(sp, passed)
                if isinstance(t, int) and t == NT - 1:
                    sp.dma_start(out[LAST + P - NEW:ROWS, :], y[P - NEW:P, par, :]).then_inc(out_ok[par], 16)
                else:
                    sp.dma_start(out[bass.ds(t * P, P), :], y[:, par, :]).then_inc(out_ok[par], 16)

            load_a(0, 0)

            def step(t, par, has):
                if has["a"]:
                    load_h(t + 1, 1 - par)
                if not isinstance(t, int) or t + 2 < NT:
                    if not isinstance(t, int) or t + 2 >= 1:
                        load_a(t + 2, par)
                if has["f"]:
                    store(t - 1, 1 - par)

            steps(sp, step)
            for q in out_ok:
                sp.wait_ge(q, 16 * NT // 2)

        @block.gpsimd
        def _(pool):
            chain = Chain(pool, pool_c)
            chain(pool.memset(ident[:], 0.0))
            pool.affine_select(out=ident[:], in_=ident[:], compare_op=ALU.not_equal, fill=1.0, base=0,
                               pattern=[[-1, P]], channel_multiplier=1).then_inc(const_ok, 1)
            pool.wait_ge(bias_in, 16)

            def step(t, par, has):
                if has["o"]:
                    pool.wait_ge(o_read, 2 * t + 2)
                    wait(pool, f_read, 2 * (t - 1))
                    pool.tensor_tensor(hb[:, par, :], h2[:], bias_sb[:], ALU.add).then_inc(hb_done, 1)

            steps(pool, step)

        @block.scalar
        def _(act):
            def split(n, filled, hi_sem, dst, first):
                for h in range(2):
                    act.wait_ge(filled, n + h + 1)
                    act.copy(dst[:, 4 * h:4 * h + 4, :].rearrange("p c j -> p (c j)"),
                             psT[first + h][:]).then_inc(hi_sem, 1)

            def step(t, par, has):
                if has["f"]:
                    split(2 * (t - 1), x_filled, x_hi, xth, 0)
                if has["a"]:
                    split(2 * (t + 1), a_filled, a_hi, ath, 2)

            steps(act, step)

        @block.vector
        def _(dve):
            def split(n, hi_sem, lo_sem, hi, lo, first):
                for h in range(2):
                    dve.wait_ge(hi_sem, n + h + 1)
                    c = slice(4 * h, 4 * h + 4)
                    dve.tensor_tensor(lo[:, c, :].rearrange("p c j -> p (c j)"), psT[first + h][:],
                                      hi[:, c, :].rearrange("p c j -> p (c j)"), ALU.subtract).then_inc(lo_sem, 1)

            LINKS = 15

            def step(t, par, has):
                if has["f"]:
                    split(2 * (t - 1), x_hi, x_lo, xth, xtl, 0)
                if has["o"]:
                    dve.wait_ge(h_arr[par], 8 * (t - par) + 16)
                    wait(dve, hb_done, t)
                    for h in range(2):
                        c = slice(h * HALF, (h + 1) * HALF)
                        dve.wait_ge(o_filled, 2 * t + h + 1)
                        dve.scalar_tensor_tensor(h2[:, c], psO[h][:], osc[:, 2:3], h_in[:, par, c],
                                                 ALU.mult, ALU.add).then_inc(o_read, 1)
                    dve.wait_ge(o_read, 2 * t + 2)
                    chain = Chain(dve, ln_c)
                    chain.base = LINKS * t
                    for h in range(2):
                        chain(dve.bn_stats(stats[:, h, :], h2[:, h * HALF:(h + 1) * HALF]), passed)
                    chain(dve.bn_aggr(mv[:], stats[:]))
                    rsqrt(dve, chain, rs, mv[:, 1:2])
                    assert chain.n == LINKS, chain.n
                    wait(dve, x_filled, 2 * t)
                    dve.tensor_scalar(xh[:], h2[:], mv[:, 0:1], rs[:, 3, :], ALU.subtract, ALU.mult).then_inc(ln_done, 1)
                if has["a"]:
                    split(2 * (t + 1), a_hi, a_lo, ath, atl, 2)
                if has["f"]:
                    dve.wait_ge(hb_done, t)
                    if not isinstance(t, int) or t >= 3:
                        dve.wait_ge(out_ok[1 - par], 8 * (t - 1 - (1 - par)))
                    for h in range(2):
                        c = slice(h * HALF, (h + 1) * HALF)
                        dve.wait_ge(f_filled, 2 * (t - 1) + h + 1)
                        dve.scalar_tensor_tensor(y[:, 1 - par, c], psF[h][:], fsc[:, 1:2], hb[:, 1 - par, c],
                                                 ALU.mult, ALU.add).then_inc(f_read, 1)

            steps(dve, step)

        @block.tensor
        def _(pe):
            pe.wait_ge(const_ok, 1)

            def turn(src, first, filled, lo_sem, n):
                for h in range(2):
                    wait(pe, lo_sem, n - 1 + h)
                    for k in range(4):
                        c = (4 * h + k) * P
                        m = pe.transpose(psT[first + h][:, k * P:(k + 1) * P], src[:, c:c + P], ident[:])
                    m.then_inc(filled, 1)

            def project(ps, th, tl, wh, wl, filled):
                for h in range(2):
                    c = slice(h * HALF, (h + 1) * HALF)
                    for k in range(KC):
                        pe.matmul(ps[h][:], th[:, k, :], wh[:, k, c], start=k == 0, stop=False)
                        pe.matmul(ps[h][:], th[:, k, :], wl[:, k, c], start=False, stop=False)
                        m = pe.matmul(ps[h][:], tl[:, k, :], wh[:, k, c], start=False, stop=k == KC - 1)
                    m.then_inc(filled, 1)

            def step(t, par, has):
                if has["f"]:
                    pe.wait_ge(ln_done, t)
                    turn(xh, 0, x_filled, x_lo, 2 * (t - 1))
                if has["o"]:
                    pe.wait_ge(a_lo, 2 * t + 2)
                    wait(pe, o_read, 2 * t)
                    project(psO, ath, atl, woh, wol, o_filled)
                if has["a"]:
                    pe.wait_ge(a_arr[1 - par], 8 * (t + 1 - (1 - par)) + 16)
                    turn(a_in[:, 1 - par, :], 2, a_filled, a_lo, 2 * (t + 1))
                if has["f"]:
                    pe.wait_ge(x_lo, 2 * t)
                    wait(pe, f_read, 2 * (t - 1))
                    project(psF, xth, xtl, wfh, wfl, f_filled)

            steps(pe, step)


def build(nc, x, txt, log_dt, lam, wq, wk, wv, wo, w_base, b_base, enc0, enc1, coefs0, coefs1, mask0, mask1,
          fourier, out, hcat, acat):
    with nc.semaphore("txt_in") as txt_in, nc.Block() as block:
        @block.scalar
        def _(act):
            act.dma_start(hcat.rearrange("(c s) d -> c s d", s=S)[:, H:S, :], txt).then_inc(txt_in, 16)
            act.wait_ge(txt_in, 16)

    ssm(nc, x, log_dt, lam, hcat)
    with ExitStack() as ctx:
        sb = lambda n, s, d=F16: ctx.enter_context(nc.sbuf_tensor(n, s, d))
        ksc = sb("ksc", [P, 4], F32)
        with ExitStack() as inner:
            sb3 = lambda n, s, d=F16: inner.enter_context(nc.sbuf_tensor(n, s, d))
            qh, ql = sb3("qh", [P, KC, QW]), sb3("ql", [P, KC, QW])
            kh, kl = sb3("kh", [P, KC, 2 * KW]), sb3("kl", [P, KC, 2 * KW])
            qsc, escale = sb3("qsc", [P, 4], F32), sb3("escale", [P, 1], F32)
            prep_qkv(nc, wq, wk, wv, qh, ql, kh, kl, qsc, ksc, escale)
            attention(nc, hcat, acat, qh, ql, kh, kl, escale)
        woh, wol, wfh, wfl = (sb(n, [P, KC, D]) for n in ("woh", "wol", "wfh", "wfl"))
        osc, fsc = sb("osc", [P, 4], F32), sb("fsc", [P, 4], F32)
        prep_out(nc, wo, w_base, enc0, enc1, (coefs0, coefs1), (mask0, mask1), fourier,
                 woh, wol, wfh, wfl, osc, fsc, ksc)
        output(nc, hcat, acat, b_base, out, woh, wol, wfh, wfl, osc, fsc)


def fourier_matrix(n):
    o = np.arange(n, dtype=np.float64)
    m = np.zeros((n, n))
    m[0] = 1.0 / np.sqrt(n)
    for k in range(1, (n - 1) // 2 + 1):
        m[2 * k - 1] = np.sqrt(2.0 / n) * np.cos(2 * np.pi * ((k * o) % n) / n)
        m[2 * k] = np.sqrt(2.0 / n) * np.sin(2 * np.pi * ((k * o) % n) / n)
    m[n - 1] = (1.0 - 2.0 * (o % 2)) / np.sqrt(n)
    return m.astype(np.float32)


_INS = ["x", "txt", "L0_tok_log_dt", "L0_tok_Lambda", "L0_attn_wq", "L0_attn_wk", "L0_attn_wv", "L0_attn_wo",
        "L0_ffn_W_base", "L0_ffn_b_base", "L0_ffn_enc0", "L0_ffn_enc1", "L0_ffn_coefs0", "L0_ffn_coefs1",
        "L0_ffn_mask0", "L0_ffn_mask1"]


def kernel(**inputs):
    import concourse.bacc as bacc
    from concourse.bass_utils import run_bass_kernel_spmd

    nc = bacc.Bacc("TRN2", target_bir_lowering=False, num_devices=1)
    arrays, args = {}, []
    for name in _INS:
        a = np.ascontiguousarray(inputs[name])
        if a.dtype == np.bool_:
            a = a.astype(np.int32)
        arrays[f"in_{name}"] = a
        args.append(nc.dram_tensor(f"in_{name}", a.shape, mybir.dt.from_np(a.dtype), kind="ExternalInput").ap())
    arrays["in_fourier"] = fourier_matrix(D)
    args.append(nc.dram_tensor("in_fourier", (D, D), F32, kind="ExternalInput").ap())
    args.append(nc.dram_tensor("out_0", (ROWS, D), F32, kind="ExternalOutput").ap())
    args.append(nc.dram_tensor("hcat", (ROWS, D), F32, kind="Internal").ap())
    args.append(nc.dram_tensor("acat", (ROWS, D), F32, kind="Internal").ap())
    build(nc, *args)
    r = run_bass_kernel_spmd(nc, [arrays], core_ids=[0])
    return r.results[0]["out_0"].reshape(B, S, D)
```

```python
from contextlib import ExitStack

import numpy as np

import concourse.bass as bass
from concourse import mybir

F32 = mybir.dt.float32
F16 = mybir.dt.float16
BF16 = mybir.dt.bfloat16
I32 = mybir.dt.int32
ALU = mybir.AluOpType
ACT = mybir.ActivationFunctionType
AX = mybir.AxisListType
RMAX = bass.bass_isa.ReduceOp.max

P = 128
B = 32
H = 128
N = 64
L = 1024
D = 1024
TXT = 77
S = H + TXT
ROWS = B * S
KC = D // P
NH, NKV, HD = 32, 8, 32
REP = NH // NKV
QW, KW = NH * HD, NKV * HD
R0, R1, E = 32, 8, 3
R = R0 + R1
ROUND = 12582912.0
TWO_PI = 6.283185
LA, LB = 4, L // 4
HC = 8
MROW = 32768.0
STACK = 3 * HD
TOP = {"q": 4.0, "k": 2.0, "o": 8.0, "f": 8.0}
EPS_LN = 1e-5
SMALL_LOADS = 4 * E + 2


def wait(eng, sem, value):
    if isinstance(value, int) and value <= 0:
        return
    eng.wait_ge(sem, value)


class Chain:

    def __init__(self, eng, sem):
        self.eng, self.sem, self.base, self.n = eng, sem, 0, 0

    def __call__(self, ins, passed=None):
        ins.then_inc(self.sem, 1)
        self.n += 1
        self.eng.wait_ge(self.sem, self.base + self.n)
        if passed is not None:
            pass_on(self.eng, passed)


def pass_on(eng, passed):
    eng.sem_inc(passed, 1)


def ssm(nc, x, txt, log_dt, lam, hcat, ahead, peak):
    NCH = H // HC
    with ExitStack() as ctx:
        sb = lambda n, s, d=F32: ctx.enter_context(nc.sbuf_tensor(n, s, d))
        sem = lambda n: ctx.enter_context(nc.semaphore(n))
        wr = sb("wr", [P, B, H])
        wi = sb("wi", [P, B, H])
        ident = sb("ident1", [P, P])
        lam_sb = sb("lam_sb", [P, 2])
        ldt = sb("ldt", [P, H, 2])
        dt = sb("dt", [P, H, 2])
        g = sb("g", [P, 1])
        sgn = sb("sgn", [P, 1])
        lbg = sb("lbg", [P, 1])
        lag = sb("lag", [P, 1])
        phi = sb("phi", [P, 1])
        a = sb("a", [P, H])
        b = sb("b", [P, H])
        f = sb("f", [P, H])
        args = sb("args", [P, 2, 2, H])
        turns = sb("turns", [P, 3, 2 * H])
        whole = sb("whole", [P, 3, 2 * H])
        trig = sb("trig", [P, 3, 2 * H])
        ex = sb("ex", [P, 2 * H])
        th = sb("th", [P, 2 * H])
        t1 = sb("t1", [P, 2 * H])
        t2 = sb("t2", [P, 2 * H])
        em = sb("em", [P, 2, 2, H])
        cc = sb("cc", [P, 8, H])
        ilb = sb("ilb", [P, LB])
        ila = sb("ila", [P, LA])
        fla = sb("fla", [P, 2, LA, H])
        tla = sb("tla", [P, 2, LA, H])
        wla = sb("wla", [P, 2, LA, H])
        ela = sb("ela", [P, LA, H])
        gg = sb("gg", [P, 2, LA, H])
        tA = sb("tA", [P, LA, H])
        tt = sb("tt", [P, HC, LB])
        tw = sb("tw", [P, HC, LB])
        es = sb("es", [P, 2, HC, LB])
        mag = sb("mag", [P, 2, HC, LB])
        x_sb = mag[:].rearrange("p k j l -> p (k j l)").rearrange("p (c m) -> p c m", m=2 * N)
        u = sb("u", [P, 2, HC, LA, B])
        u2 = sb("u2", [P, 2, HC, LA, B])
        ob = sb("ob", [P, 2, HC, LB])
        ps = [ctx.enter_context(nc.psum_tensor(f"ps1_{i}", [P, 2, LB], F32)) for i in range(4)]
        pt = [ctx.enter_context(nc.psum_tensor(f"pt1_{i}", [P, 4, P], F32)) for i in range(2)]
        twice = [t[:].rearrange("p k j l -> p (k j l)").rearrange("p (c m) -> p c m", m=P) for t in (ob, es)]
        twice_ok = sem("twice_ok")
        in_small, in_x, txt_in = sem("in_small"), sem("in_x"), sem("txt_in")
        pool_c, dve_c = sem("pool_c"), sem("dve_c")
        ready, act_c = sem("ready"), sem("act_c")
        iota_ok, ident_ok = sem("iota_ok"), sem("ident_ok")
        xt_filled, xt_read = sem("xt_filled"), sem("xt_read")
        reduced, sin_ok, mag_ok, e_ok = sem("reduced"), sem("sin_ok"), sem("mag_ok"), sem("e_ok")
        gg_ok, u2_ok = sem("gg_ok"), sem("u2_ok")
        u_ok, mm_done, k_read = sem("u_ok"), sem("mm_done"), sem("k_read")
        stored = [sem("stored0"), sem("stored1")]

        def by_mode(w, ch):
            v = w[:, :, ch * HC:(ch + 1) * HC].rearrange("p c h -> p h c")
            return v.unsqueeze(2).broadcast_to([P, HC, LA, B])

        def by_place(k, ch):
            v = gg[:, k, :, ch * HC:(ch + 1) * HC].rearrange("p a h -> p h a")
            return v.unsqueeze(3).broadcast_to([P, HC, LA, B])

        hview = hcat.rearrange("(c s) (la lb) -> la c s lb", s=S, lb=LB)
        block = ctx.enter_context(nc.Block())

        @block.sync
        def _(sp):
            sp.dma_start(lam_sb[0:N, :], lam).then_inc(in_small, 16)
            sp.dma_start(lam_sb[N:P, :], lam).then_inc(in_small, 16)
            sp.dma_start(ldt[:], log_dt.rearrange("(o h) t -> o h t", o=1).broadcast_to([P, H, 2])).then_inc(in_small, 16)
            sp.dma_start(x_sb, x.rearrange("c h n t -> h c (n t)")).then_inc(in_x, 16)
            sp.dma_start(ahead[0], ahead[1]).then_inc(ahead[2], 16)
            for ch in range(NCH):
                sp.wait_ge(k_read, (ch + 1) * HC // 2)
                for la in range(LA):
                    sp.dma_start(hview[la, :, ch * HC:(ch + 1) * HC, :],
                                 ob[la * B:(la + 1) * B, ch % 2, :, :]).then_inc(stored[ch % 2], 16)
            for q in range(2):
                sp.wait_ge(stored[q], 16 * LA * NCH // 2)

        @block.gpsimd
        def _(pool):
            chain = Chain(pool, pool_c)
            pool.iota(ilb[:], pattern=[[1, LB]], base=0, channel_multiplier=0,
                      allow_small_or_imprecise_dtypes=True).then_inc(iota_ok, 1)
            pool.iota(ila[:], pattern=[[LB, LA]], base=0, channel_multiplier=0,
                      allow_small_or_imprecise_dtypes=True).then_inc(iota_ok, 1)
            chain(pool.memset(ident[:], 0.0))
            pool.affine_select(out=ident[:], in_=ident[:], compare_op=ALU.not_equal, fill=1.0, base=0,
                               pattern=[[-1, P]], channel_multiplier=1).then_inc(ident_ok, 1)
            pool.wait_ge(gg_ok, 1)
            for ch in range(NCH):
                if ch >= 2:
                    pool.wait_ge(u_ok, ch - 1)
                pool.tensor_tensor(u2[:, ch % 2], by_mode(wi, ch), by_place(1, ch), ALU.mult).then_inc(u2_ok, 1)
                pool.wait_ge(sin_ok, ch + 1)
                pool.wait_ge(mag_ok, ch + 1)
                pool.tensor_tensor(es[:, ch % 2], es[:, ch % 2], mag[:, ch % 2], ALU.mult).then_inc(e_ok, 1)

        @block.scalar
        def _(act):
            act.wait_ge(in_x, 16)
            for t in range(2):
                part = x_sb.rearrange("p c (n t) -> p c n t", t=2)[:, :, :, t]
                for k in range(2):
                    act.copy(twice[t][:, :, k * N:(k + 1) * N], part).then_inc(twice_ok, 1)
            act.wait_ge(in_small, 48)
            act.activation(dt[:], ldt[:], ACT.Exp).then_inc(act_c, 1)
            act.wait_ge(ready, 1)
            act.activation(ex[:], args[:, 0].rearrange("p k h -> p (k h)"), ACT.Exp).then_inc(act_c, 1)
            act.activation(th[:], args[:, 0].rearrange("p k h -> p (k h)"), ACT.Tanh, scale=0.5).then_inc(act_c, 1)
            act.activation(trig[:], turns[:], ACT.Sin, scale=TWO_PI).then_inc(act_c, 1)
            act.wait_ge(ready, 2)
            act.activation(tla[:], wla[:], ACT.Sin, scale=TWO_PI).then_inc(act_c, 1)
            act.activation(ela[:], fla[:, 0], ACT.Exp).then_inc(act_c, 1)
            act.dma_start(hcat.rearrange("(c s) d -> c s d", s=S)[:, H:S, :], txt).then_inc(txt_in, 16)

            def results(ch):
                for j in range(HC // 2):
                    n = ch * HC // 2 + j
                    act.wait_ge(mm_done, n + 1)
                    if j == 0 and ch >= 2:
                        act.wait_ge(stored[ch % 2], 16 * LA * (ch // 2))
                    act.copy(ob[:, ch % 2, 2 * j:2 * j + 2, :], ps[n % 4][:]).then_inc(k_read, 1)

            act.wait_ge(xt_filled, 2 * B // 4)
            for ch in range(NCH):
                if ch >= 2:
                    act.wait_ge(mm_done, (ch - 1) * HC // 2)
                for j in range(HC):
                    h = ch * HC + j
                    m = act.activation(mag[:, ch % 2, j, :], ilb[:], ACT.Exp, scale=a[:, h:h + 1])
                m.then_inc(mag_ok, 1)
                act.wait_ge(reduced, ch + 1)
                act.activation(es[:, ch % 2], tw[:], ACT.Sin, scale=TWO_PI).then_inc(sin_ok, 1)
                if ch:
                    results(ch - 1)
            results(NCH - 1)
            act.wait_ge(txt_in, 16)

        @block.vector
        def _(dve):
            chain = Chain(dve, dve_c)
            dve.memset(phi[0:N, :], 0.25)
            dve.memset(phi[N:P, :], 0.0)
            dve.wait_ge(in_small, 48)
            lr, li = lam_sb[:, 0:1], lam_sb[:, 1:2]
            chain(dve.tensor_scalar(g[:], lr, 0.0, None, ALU.is_gt))
            chain(dve.tensor_scalar(sgn[:], g[:], -2.0, 1.0, ALU.mult, ALU.add))
            dve.tensor_scalar(lag[:], g[:], -float(LB * (LA - 1)), None, ALU.mult)
            chain(dve.tensor_scalar(lbg[:], g[:], -float(LB - 1), None, ALU.mult))
            dve.wait_ge(iota_ok, 2)
            chain(dve.tensor_scalar(ilb[:], ilb[:], lbg[:, 0:1], None, ALU.add))
            chain(dve.tensor_scalar(ila[:], ila[:], lag[:, 0:1], None, ALU.add))
            dve.wait_ge(act_c, 1)
            chain(dve.tensor_scalar(a[:], dt[:, :, 0], lr, None, ALU.mult))
            chain(dve.tensor_scalar(b[:], dt[:, :, 1], li, None, ALU.mult))
            for k, src in enumerate((a, b)):
                chain(dve.tensor_scalar(args[:, k, 0, :], src[:], sgn[:, 0:1], None, ALU.mult))
                chain(dve.tensor_scalar(args[:, k, 1, :], args[:, k, 0, :], float(L), None, ALU.mult))
            bb = args[:, 1].rearrange("p k h -> p (k h)")
            tp = 1.0 / (2.0 * np.pi)
            chain(dve.tensor_scalar(turns[:, 0, :], bb, tp, None, ALU.mult))
            chain(dve.tensor_scalar(turns[:, 1, :], turns[:, 0, :], 0.25, None, ALU.add))
            chain(dve.tensor_scalar(turns[:, 2, :], turns[:, 0, :], 0.5, None, ALU.mult))
            chain(dve.tensor_scalar(whole[:], turns[:], ROUND, None, ALU.add))
            chain(dve.tensor_scalar(whole[:], whole[:], ROUND, None, ALU.subtract))
            dve.tensor_tensor(turns[:], turns[:], whole[:], ALU.subtract).then_inc(ready, 1)
            chain(dve.tensor_scalar(f[:], b[:], tp, None, ALU.mult))
            for la in range(LA):
                chain(dve.tensor_scalar(fla[:, 0, la, :], a[:], ila[:, la:la + 1], None, ALU.mult))
                chain(dve.tensor_scalar(tla[:, 0, la, :], f[:], ila[:, la:la + 1], None, ALU.mult))
                chain(dve.tensor_scalar(tla[:, 1, la, :], tla[:, 0, la, :], 0.25, None, ALU.add))
            chain(dve.tensor_scalar(wla[:], tla[:], ROUND, None, ALU.add))
            chain(dve.tensor_scalar(wla[:], wla[:], ROUND, None, ALU.subtract))
            dve.tensor_tensor(wla[:], tla[:], wla[:], ALU.subtract).then_inc(ready, 1)
            dve.wait_ge(act_c, 4)
            chain(dve.scalar_tensor_tensor(t1[:], ex[:], 1.0, th[:], ALU.add, ALU.mult))
            chain(dve.tensor_tensor(t1[:], t1[:], trig[:, 1, :], ALU.mult))
            chain(dve.scalar_tensor_tensor(t2[:], trig[:, 2, :], -2.0, trig[:, 2, :], ALU.mult, ALU.mult))
            chain(dve.tensor_tensor(em[:, 0].rearrange("p k h -> p (k h)"), t1[:], t2[:], ALU.add))
            chain(dve.tensor_tensor(em[:, 1].rearrange("p k h -> p (k h)"), ex[:], trig[:, 0, :], ALU.mult))
            c = lambda i: cc[:, i, :]
            chain(dve.tensor_scalar(c(0), em[:, 1, 1, :], li, None, ALU.mult))
            chain(dve.scalar_tensor_tensor(c(1), em[:, 0, 1, :], lr, c(0), ALU.mult, ALU.subtract))
            chain(dve.tensor_scalar(c(2), em[:, 1, 1, :], lr, None, ALU.mult))
            chain(dve.scalar_tensor_tensor(c(3), em[:, 0, 1, :], li, c(2), ALU.mult, ALU.add))
            chain(dve.tensor_tensor(c(4), c(1), c(1), ALU.mult))
            chain(dve.tensor_tensor(c(5), c(3), c(3), ALU.mult))
            chain(dve.scalar_tensor_tensor(c(4), c(4), 1e-7, c(5), ALU.add, ALU.add))
            chain(dve.reciprocal(c(5), c(4)))
            chain(dve.tensor_tensor(c(1), c(1), c(5), ALU.mult))
            chain(dve.scalar_tensor_tensor(c(3), c(3), -1.0, c(5), ALU.mult, ALU.mult))
            chain(dve.tensor_tensor(c(4), em[:, 0, 0, :], c(1), ALU.mult))
            chain(dve.tensor_tensor(c(5), em[:, 1, 0, :], c(3), ALU.mult))
            chain(dve.tensor_tensor(c(6), c(4), c(5), ALU.subtract))
            chain(dve.tensor_tensor(c(4), em[:, 0, 0, :], c(3), ALU.mult))
            chain(dve.tensor_tensor(c(5), em[:, 1, 0, :], c(1), ALU.mult))
            chain(dve.tensor_tensor(c(7), c(4), c(5), ALU.add))
            dve.wait_ge(act_c, 6)
            chain(dve.tensor_tensor(tla[:, 0], tla[:, 0], ela[:], ALU.mult))
            chain(dve.tensor_tensor(tla[:, 1], tla[:, 1], ela[:], ALU.mult))
            cr = cc[:, 6:7, :].broadcast_to([P, LA, H])
            ci = cc[:, 7:8, :].broadcast_to([P, LA, H])
            chain(dve.tensor_tensor(fla[:, 0], tla[:, 1], cr, ALU.mult))
            chain(dve.tensor_tensor(tA[:], tla[:, 0], ci, ALU.mult))
            chain(dve.tensor_tensor(fla[:, 0], fla[:, 0], tA[:], ALU.subtract))
            chain(dve.tensor_tensor(fla[:, 1], tla[:, 0], cr, ALU.mult))
            chain(dve.tensor_tensor(tA[:], tla[:, 1], ci, ALU.mult))
            chain(dve.tensor_tensor(fla[:, 1], fla[:, 1], tA[:], ALU.add))
            chain(dve.tensor_copy(gg[0:N, 0], fla[0:N, 0]))
            chain(dve.tensor_scalar(gg[N:P, 0], fla[N:P, 1], -1.0, None, ALU.mult))
            chain(dve.tensor_scalar(gg[0:N, 1], fla[0:N, 1], -1.0, None, ALU.mult))
            chain(dve.tensor_scalar(gg[N:P, 1], fla[N:P, 0], -1.0, None, ALU.mult))
            for n in range(2 * B // 4):
                dve.wait_ge(xt_filled, n + 1)
                dst = (wr if n % 2 == 0 else wi)[:, 4 * (n // 2):4 * (n // 2) + 4, :]
                chain(dve.tensor_copy(dst, pt[n % 2][:]))
                dve.sem_inc(xt_read, 1)
            dve.sem_inc(gg_ok, 1)
            for ch in range(NCH):
                if ch:
                    dve.wait_ge(sin_ok, ch)
                for j in range(HC):
                    h = ch * HC + j
                    m = dve.tensor_scalar(tt[:, j, :], ilb[:], f[:, h:h + 1], phi[:, 0:1], ALU.mult, ALU.add)
                chain(m)
                chain(dve.tensor_scalar(tw[:], tt[:], ROUND, ROUND, ALU.add, ALU.subtract))
                if ch >= 2:
                    dve.wait_ge(mm_done, (ch - 1) * HC // 2)
                dve.tensor_tensor(tw[:], tt[:], tw[:], ALU.subtract).then_inc(reduced, 1)
                chain(dve.tensor_tensor(u[:, ch % 2], by_mode(wr, ch), by_place(0, ch), ALU.mult))
                dve.wait_ge(u2_ok, ch + 1)
                dve.tensor_tensor(u[:, ch % 2], u[:, ch % 2], u2[:, ch % 2], ALU.add).then_inc(u_ok, 1)
                dve.wait_ge(u_ok, ch + 1)
            dve.wait_ge(ahead[2], 16)
            dve.tensor_reduce(peak[:], ahead[0].rearrange("p k n -> p (k n)"), AX.X, ALU.max,
                              apply_absolute_value=True)

        @block.tensor
        def _(pe):
            pe.wait_ge(twice_ok, 4)
            pe.wait_ge(ident_ok, 1)
            for n in range(2 * B // 4):
                if n >= 2:
                    pe.wait_ge(xt_read, n - 1)
                for k in range(4):
                    cb = 4 * (n // 2) + k
                    m = pe.transpose(pt[n % 2][:, k, :], twice[n % 2][:, cb, :], ident[:])
                m.then_inc(xt_filled, 1)
            for ch in range(NCH):
                pe.wait_ge(u_ok, ch + 1)
                pe.wait_ge(e_ok, ch + 1)
                for j in range(HC):
                    n = (ch * HC + j) // 2
                    if j % 2 == 0 and n >= 4:
                        pe.wait_ge(k_read, n - 3)
                    m = pe.matmul(ps[n % 4][:, j % 2, :], u[:, ch % 2, j].rearrange("p a c -> p (a c)"),
                                  es[:, ch % 2, j, :], start=True, stop=True)
                    if j % 2:
                        m.then_inc(mm_done, 1)


def scale_and_split(nc, ctx, tag, jobs):
    return {k: ctx.enter_context(nc.semaphore(f"{tag}_{k}")) for k in
            ("loaded", "peak", "all_peak", "scale", "hi", "lo", "chain", "made")}


def weight_scales(dve, chain, peak, sc, top):
    chain(dve.tensor_scalar(sc[:, 2:3], peak, 1e-30, None, ALU.max))
    chain(dve.tensor_scalar(sc[:, 3:4].bitcast(I32), sc[:, 2:3].bitcast(I32), 0x7F800000, None, ALU.bitwise_and))
    chain(dve.reciprocal(sc[:, 2:3], sc[:, 3:4]))
    chain(dve.tensor_scalar(sc[:, 0:1], sc[:, 2:3], top, None, ALU.mult))
    chain(dve.tensor_scalar(sc[:, 1:2], sc[:, 3:4], 1.0 / top, None, ALU.mult))


def prep_qkv(nc, stage, peak_q, wk, wv, qh, ql, kh, kl, qsc, ksc, escale):
    with ExitStack() as ctx:
        sb = lambda n, s, d=F32: ctx.enter_context(nc.sbuf_tensor(n, s, d))
        st = [stage, sb("st_k", [P, KC, 2 * KW])]
        peaks = (peak_q, sb("peak_k", [P, 1]))
        apeak = sb("apeak", [P, 2])
        s = scale_and_split(nc, ctx, "p2", 2)
        s_k = ctx.enter_context(nc.semaphore("p2_loaded_k"))
        hi, lo, scs, tops = (qh, kh), (ql, kl), (qsc, ksc), (TOP["q"], TOP["k"])
        block = ctx.enter_context(nc.Block())

        @block.sync
        def _(sp):
            sp.dma_start(st[1][:, :, 0:KW], wk.rearrange("(k p) n -> p k n", p=P)).then_inc(s_k, 16)
            sp.dma_start(st[1][:, :, KW:2 * KW], wv.rearrange("(k p) n -> p k n", p=P)).then_inc(s_k, 16)

        @block.gpsimd
        def _(pool):
            for n in range(2):
                if n:
                    pool.wait_ge(s["peak"], n)
                pool.partition_all_reduce(apeak[:, n:n + 1], peaks[n][:], P, RMAX).then_inc(s["all_peak"], 1)

        @block.scalar
        def _(act):
            for n in range(2):
                act.wait_ge(s["scale"], n + 1)
                for k in range(KC):
                    act.activation(hi[n][:, k], st[n][:, k], ACT.Copy, scale=scs[n][:, 0:1]).then_inc(s["hi"], 1)

        @block.vector
        def _(dve):
            chain = Chain(dve, s["chain"])
            for n in range(2):
                if n:
                    dve.wait_ge(s_k, 32)
                    dve.tensor_reduce(peaks[1][:], st[1][:].rearrange("p k n -> p (k n)"), AX.X, ALU.max,
                                      apply_absolute_value=True).then_inc(s["peak"], 1)
                dve.wait_ge(s["all_peak"], n + 1)
                weight_scales(dve, chain, apeak[:, n:n + 1], scs[n], tops[n])
                dve.sem_inc(s["scale"], 1)
            chain(dve.scalar_tensor_tensor(escale[:], qsc[:, 1:2], float(HD) ** -0.5, ksc[:, 1:2], ALU.mult, ALU.mult))
            for n in range(2):
                for k in range(KC):
                    dve.wait_ge(s["hi"], n * KC + k + 1)
                    dve.scalar_tensor_tensor(lo[n][:, k], st[n][:, k], scs[n][:, 0:1], hi[n][:, k],
                                             ALU.mult, ALU.subtract)


def attention(nc, ahead, hcat, acat, qh, ql, kh, kl, escale):
    T = (P, TXT)
    with ExitStack() as ctx:
        sb = lambda n, s, d=F32: ctx.enter_context(nc.sbuf_tensor(n, s, d))
        sem = lambda n: ctx.enter_context(nc.semaphore(n))
        ident = sb("ident3", [P, P])
        ident_bf = sb("ident_bf", [P, P], BF16)
        mask = sb("mask", [P, REP, P], BF16)
        xin = sb("xin", [P, 2, 2, D])
        xth, xtl = sb("xth", [P, 2, KC, S], F16), sb("xtl", [P, 2, KC, S], F16)
        qsh, qsl = sb("qsh", [P, KC, S], F16), sb("qsl", [P, KC, S], F16)
        ksh, ksl = sb("ksh", [P, 2, S], F16), sb("ksl", [P, 2, S], F16)
        vsh, vsl = sb("vsh", [P, 2, NKV, HD + 1], F16), sb("vsl", [P, 2, NKV, HD + 1], F16)
        mh, ml = sb("mh", [NH, S], F16), sb("ml", [NH, S], F16)
        qst = [sb(f"qst{i}", [STACK + 2, NH, S], F16) for i in range(2)]
        kst = [sb(f"kst{i}", [STACK + 2, NKV, S], F16) for i in range(2)]
        vh = [sb(f"vh{i}", [P, 2, NKV, HD + 1], F16) for i in range(2)]
        vl = [sb(f"vl{i}", [P, 2, NKV, HD + 1], F16) for i in range(2)]
        p32 = sb("p32", [P, 2, 3, 2 * S])
        ph = sb("ph", [P, 2, 3, 2 * S], F16)
        pl = sb("pl", [P, 2, 3, 2 * S], F16)
        mx = sb("mx", [P, 2, NH])
        rden = sb("rden", [P, 2, REP])
        ao = sb("ao", [P, 2, 2, D])
        stats = sb("stats", [P, 2, 2, 6])
        mv = sb("mv", [P, 2, 2])
        rs = sb("rs", [P, 4, 2])
        psS = [ctx.enter_context(nc.psum_tensor(f"psS{i}", [P, 512], F32)) for i in range(2)]
        psT = [ctx.enter_context(nc.psum_tensor(f"psT{i}", [P, 512], F32)) for i in range(2)]
        psO = [ctx.enter_context(nc.psum_tensor(f"psO{i}", [P, 2, REP, HD + 1], F32)) for i in range(2)]
        psJ = [ctx.enter_context(nc.psum_tensor(f"psJ{i}", [P, 512], F32)) for i in range(2)]
        cleared, lo_pool = sem("cleared"), sem("lo_pool")
        passed = sem("passed3")
        pool_c, dve_c, dve_ln, const_ok = sem("pool_c3"), sem("dve_c3"), sem("dve_ln"), sem("const_ok")
        x_in, ln_done = [sem("x_in0"), sem("x_in1")], sem("ln_done")
        pj_filled, pj_hi, pj_lo = sem("pj_filled"), sem("pj_hi"), sem("pj_lo")
        s_filled, s_read = sem("s_filled"), sem("s_read")
        st_filled, exp_done, masked, hi_done, lo_done = (sem("st_filled"), sem("exp_done"), sem("masked"),
                                                         sem("hi_done"), sem("lo_done"))
        av_done, norm_done, rec_done = sem("av_done"), sem("norm_done"), sem("rec_done")
        q_in = [sem(f"q_in{c}") for c in range(2)]
        k_in = [sem(f"k_in{c}") for c in range(2)]
        m_in, v_in = sem("m_in"), sem("v_in")
        a_out = [sem("a_out0"), sem("a_out1")]

        SLOTS = range(NKV)
        MAXES = [[0], [1], [2], [3], [4, 5], [6, 7], [], []]
        EXTRA = {0: ("k", 0), 1: ("k", 1), 2: ("v", 0), 3: ("v", 1)}

        def units(has):
            out = []
            for s in SLOTS:
                row = []
                if has["qkv"]:
                    row.append(("q", s))
                    if s in EXTRA:
                        row.append(EXTRA[s])
                if s >= 4 and has["ln"]:
                    row.append(("x", s - 4))
                if s == NKV - 2 and has["max"]:
                    row.append(("m", 0))
                out.append(row)
            return out

        def parts(b):
            return {"att": 0 <= b < B, "last": 0 <= b - 1 < B, "max": 0 <= b + 1 < B, "qkv": 0 <= b + 2 < B, "ln": 0 <= b + 3 < B, "load": 0 <= b + 4 < B}

        def count(b):
            return sum(map(len, units(parts(b))))

        FULL = parts(2)
        PER = count(0)
        BEFORE = {b: sum(count(c) for c in range(-3, b)) for b in range(-3, B + 2)}

        def before(b, par):
            return BEFORE[b] if isinstance(b, int) else BEFORE[2] - 2 * PER + b * PER

        def odd(b, par):
            return (BEFORE[b] if isinstance(b, int) else BEFORE[2 + par]) % 2

        def at(rows, kind, n=0):
            return sum(rows, []).index((kind, n))

        def steps(eng, step):
            for b in range(-3, 2):
                step(b, b % 2, parts(b))
            with eng.Fori(1, 14) as i:
                step(i * 2, 0, FULL)
                step(i * 2 + 1, 1, FULL)
            for b in range(28, B + 1):
                step(b, b % 2, parts(b))

        def view(t, slot, k):
            if k < 2:
                return t[:, slot, k, :].rearrange("p (h i) -> p h i", i=S)
            return t[0:TXT, slot, k, 0:REP * TXT].rearrange("p (h i) -> p h i", i=TXT)

        def ps_view(t, k):
            if k < 2:
                return t[:, 0:2 * S].rearrange("p (h i) -> p h i", i=S)
            return t[0:TXT, 0:REP * TXT].rearrange("p (h i) -> p h i", i=TXT)

        def unit_views(kind, n, bank, par):
            ps = psJ[bank]
            if kind == "q":
                return ps[:, 0:S], qsh[:, n, :], qsl[:, n, :]
            if kind == "k":
                return ps[:, 0:S], ksh[:, n, :], ksl[:, n, :]
            if kind == "v":
                r = T[n]
                return (ps[0:r, 0:KW].rearrange("p (g d) -> p g d", d=HD), vsh[0:r, n, :, 0:HD],
                        vsl[0:r, n, :, 0:HD])
            if kind == "m":
                return ps[0:NH, 0:S], mh[:], ml[:]
            t, half = divmod(n, 2)
            cols = slice(t * P, t * P + T[t])
            return (ps[:, 0:4 * T[t]].rearrange("p (c j) -> p c j", j=T[t]),
                    xth[:, 1 - par, 4 * half:4 * half + 4, cols], xtl[:, 1 - par, 4 * half:4 * half + 4, cols])

        def free_place(eng, kind, n, b):
            if kind == "q":
                wait(eng, q_in[n // 4], 16 * 12 * (b + 2))
            if kind == "k":
                wait(eng, k_in[n], 16 * 12 * (b + 2))
            if kind == "v":
                wait(eng, v_in, 32 * (b + 2))
            if kind == "m":
                wait(eng, m_in, 32 * (b + 1))

        block = ctx.enter_context(nc.Block())

        @block.sync
        def _(sp):
            def restack(parts_, dst, cs, arrived):
                for k, src in enumerate(parts_):
                    rows = dst[k * HD:(k + 1) * HD].rearrange("d (c r) i -> d c r i", r=4)
                    for r in range(4):
                        sp.dma_start(rows[:, cs, r, :], src[r * HD:(r + 1) * HD, cs, :]).then_inc(arrived, 16)

            Q_PARTS, K_PARTS = (qsh, qsh, qsl), (ksh, ksl, ksh)
            HALVES = (slice(0, KC // 2), slice(KC // 2, KC))

            def step(b, par, has):
                base = before(b, par)
                rows = units(has)
                early = isinstance(b, int)
                nxt = 1 - par
                if has["max"]:
                    wait(sp, st_filled, 24 * b)
                    pass_on(sp, passed)
                    prev = parts(b - 1) if early else FULL
                    wait(sp, pj_lo, before(b - 1, nxt) + at(units(prev), "q", NKV - 1) + 1)
                    restack(K_PARTS, kst[nxt], slice(1, 2), k_in[1])
                    restack(Q_PARTS, qst[nxt], HALVES[1], q_in[1])
                if has["load"]:
                    wait(sp, pj_filled, base)
                    pass_on(sp, passed)
                    load(b + 4, par)
                if has["max"]:
                    wait(sp, av_done, 8 * b)
                    pass_on(sp, passed)
                    sp.dma_start(vh[nxt][:], vsh[:]).then_inc(v_in, 16)
                    sp.dma_start(vl[nxt][:], vsl[:]).then_inc(v_in, 16)
                if early and b == -1:
                    for dst, src, arrived in ahead:
                        sp.dma_start(dst, src).then_inc(arrived, 16)
                if has["last"]:
                    store(b - 1, nxt)
                if has["qkv"]:
                    wait(sp, pj_lo, base + at(rows, "q", 3) + 1)
                    pass_on(sp, passed)
                    wait(sp, st_filled, 24 * b + 12)
                    restack(Q_PARTS, qst[par], HALVES[0], q_in[0])
                    wait(sp, pj_lo, base + at(rows, "k", 0) + 1)
                    restack(K_PARTS, kst[par], slice(0, 1), k_in[0])
                if has["max"]:
                    wait(sp, pj_lo, base + at(rows, "m") + 1)
                    sp.dma_start(qst[nxt][STACK:STACK + 1, :, :], mh[:]).then_inc(m_in, 16)
                    sp.dma_start(qst[nxt][STACK + 1:STACK + 2, :, :], ml[:]).then_inc(m_in, 16)

            def load(b, par):
                sp.dma_start(xin[:, par, 0, :], hcat[bass.ds(b * S, P), :]).then_inc(x_in[par], 16)
                sp.dma_start(xin[0:TXT, par, 1, :], hcat[bass.ds(b * S + P, TXT), :]).then_inc(x_in[par], 16)

            def store(b, par):
                sp.wait_ge(norm_done, 8 * b + 8)
                pass_on(sp, passed)
                sp.dma_start(acat[bass.ds(b * S, P), :], ao[:, par, 0, :]).then_inc(a_out[par], 16)
                sp.dma_start(acat[bass.ds(b * S + P, TXT), :], ao[0:TXT, par, 1, :]).then_inc(a_out[par], 16)

            sp.wait_ge(cleared, 1)
            load(0, 0)
            steps(sp, step)
            for q in a_out:
                sp.wait_ge(q, 32 * B // 2)

        @block.gpsimd
        def _(pool):
            chain = Chain(pool, pool_c)
            pool.memset(mv[:], 1.0)
            pool.memset(xin[:, :, 1, :], 0.0).then_inc(cleared, 1)
            chain(pool.memset(ident[:], 0.0))
            chain(pool.affine_select(out=ident[:], in_=ident[:], compare_op=ALU.not_equal, fill=1.0, base=0,
                                     pattern=[[-1, P]], channel_multiplier=1))
            chain(pool.tensor_copy(ident_bf[:], ident[:]))
            chain(pool.memset(mask[:], 0.0))
            chain(pool.affine_select(out=mask[:], in_=mask[:], compare_op=ALU.is_ge, fill=-1e38, base=0,
                                     pattern=[[0, REP], [-1, P]], channel_multiplier=1))
            for i in range(2):
                chain(pool.memset(kst[i][STACK:STACK + 2], MROW))
            chain(pool.memset(vsh[:], 0.0))
            chain(pool.memset(vsl[:], 0.0))
            chain(pool.memset(vsh[:, :, :, HD:HD + 1], 1.0))
            pool.memset(p32[:, :, 2, :], 0.0).then_inc(const_ok, 1)

            def step(b, par, has):
                if not has["att"]:
                    return
                for g in SLOTS:
                    for k in range(3):
                        pool.wait_ge(exp_done, 24 * b + 3 * g + k + 1)
                        pass_on(pool, passed)
                        v = view(p32, g % 2, k)
                        v = v[:, :, 0:P] if k < 2 else v
                        w = v.shape[2]
                        pool.affine_select(out=v, in_=v, compare_op=ALU.is_ge, fill=0.0, base=0,
                                           pattern=[[0, v.shape[1]], [1, w]],
                                           channel_multiplier=-1).then_inc(masked, 1)
                    for k in (1, 2):
                        pool.wait_ge(hi_done, 24 * b + 3 * g + k + 1)
                        pass_on(pool, passed)
                        pool.tensor_tensor(view(pl, g % 2, k), view(p32, g % 2, k), view(ph, g % 2, k),
                                           ALU.subtract).then_inc(lo_pool, 1)

            steps(pool, step)

        @block.scalar
        def _(act):
            act.wait_ge(const_ok, 1)

            def step(b, par, has):
                base, k0 = before(b, par), odd(b, par)
                rows = units(has)
                n = 0
                for g in SLOTS:
                    if has["att"]:
                        for k in range(3):
                            act.wait_ge(st_filled, 24 * b + 3 * g + k + 1)
                            if k:
                                wait(act, lo_pool, 16 * b + 2 * (g - 2) + k)
                            else:
                                wait(act, lo_done, 8 * b + g - 1)
                            act.activation(view(p32, g % 2, k), ps_view(psT[(g + k) % 2], k), ACT.Exp,
                                           scale=(escale[:, 0:1] if k < 2 else escale[0:TXT, 0:1])
                                           ).then_inc(exp_done, 1)
                        wait(act, av_done, 8 * b + g - 1)
                        for k in range(3):
                            act.wait_ge(masked, 24 * b + 3 * g + k + 1)
                            act.copy(view(ph, g % 2, k), view(p32, g % 2, k)).then_inc(hi_done, 1)
                    for kind, m in rows[g]:
                        src, hi, _ = unit_views(kind, m, (k0 + n) % 2, par)
                        act.wait_ge(pj_filled, base + n + 1)
                        free_place(act, kind, m, b)
                        if kind == "m":
                            act.mul(hi, src, -1.0 / MROW).then_inc(pj_hi, 1)
                        else:
                            act.copy(hi, src).then_inc(pj_hi, 1)
                        n += 1

            steps(act, step)

        @block.vector
        def _(dve):
            dve.wait_ge(cleared, 1)

            def norm(b, par, g):
                n = 8 * b + g
                if g == 0:
                    wait(dve, a_out[par], 16 * (b - par))
                dve.wait_ge(av_done, n + 1)
                wait(dve, norm_done, n)
                o = psO[g % 2]
                dve.reciprocal(rden[:, 0, :], o[:, 0, :, HD]).then_inc(rec_done, 1)
                dve.reciprocal(rden[0:TXT, 1, :], o[0:TXT, 1, :, HD]).then_inc(rec_done, 1)
                dve.wait_ge(rec_done, 2 * n + 2)
                for t in range(2):
                    r = T[t]
                    dst = ao[0:r, par, t, g * P:(g + 1) * P].rearrange("p (h d) -> p h d", d=HD)
                    ins = dve.tensor_tensor(dst, o[0:r, t, :, 0:HD],
                                            rden[0:r, t, :].unsqueeze(2).broadcast_to([r, REP, HD]), ALU.mult)
                ins.then_inc(norm_done, 1)

            LINKS = 20

            def layer_norm(b, par, g):
                chain = Chain(dve, dve_ln)
                chain.base = LINKS * (b + 3)
                x = xin[:, 1 - par]
                if g < 2:
                    if g == 0:
                        dve.wait_ge(x_in[1 - par], 16 * (b + 4 + par))
                    chain.n = 3 * g
                    for h in range(2):
                        chain(dve.bn_stats(stats[0:T[g], g, h, :], x[0:T[g], g, 512 * h:512 * h + 512]), passed)
                    chain(dve.bn_aggr(mv[0:T[g], g, :], stats[0:T[g], g]))
                elif g == 2:
                    chain.n = 6
                    rsqrt(dve, chain, rs, mv[:, :, 1])
                else:
                    chain.n = 18
                    for t in range(2):
                        r = T[t]
                        dve.tensor_scalar(x[0:r, t, :], x[0:r, t, :], mv[0:r, t, 0:1],
                                          rs[0:r, 3, t:t + 1], ALU.subtract, ALU.mult).then_inc(ln_done, 1)
                    dve.sem_inc(dve_ln, 2)

            def take_maxes(b, j, base, ks):
                for k in ks:
                    dve.wait_ge(s_filled, 24 * (b + 1) + 3 * j + k + 1)
                    if j == 0 and k == 0:
                        wait(dve, pj_filled, base)
                    src = psS[(j + k) % 2]
                    if k == 0:
                        v, dst = src[:].rearrange("p (h i) -> p h i", i=P), mx[:, 0, 4 * j:4 * j + 4]
                    else:
                        v = src[0:TXT, 0:2 * S].rearrange("p (h i) -> p h i", i=S)
                        dst = mx[0:TXT, 1, 4 * j + 2 * k - 2:4 * j + 2 * k]
                    dve.tensor_reduce(dst, v, AX.X, ALU.max).then_inc(s_read, 1)

            def split_unit(b, par, bank, kind, m, count_):
                src, hi, lo = unit_views(kind, m, bank, par)
                dve.wait_ge(pj_hi, count_)
                if kind == "m":
                    dve.scalar_tensor_tensor(lo, src, -1.0 / MROW, hi, ALU.mult, ALU.subtract).then_inc(pj_lo, 1)
                else:
                    dve.tensor_tensor(lo, src, hi, ALU.subtract).then_inc(pj_lo, 1)

            def step(b, par, has):
                base, k0 = before(b, par), odd(b, par)
                rows = units(has)
                n = 0
                late = None
                for g in SLOTS:
                    groups = MAXES[g] if has["max"] else []
                    for j in groups[:1]:
                        take_maxes(b, j, base, (0, 1))
                    if late:
                        split_unit(*late)
                        late = None
                    for j in groups[:1]:
                        take_maxes(b, j, base, (2,))
                    if has["att"]:
                        dve.wait_ge(hi_done, 24 * b + 3 * g + 1)
                        dve.tensor_tensor(view(pl, g % 2, 0), view(p32, g % 2, 0), view(ph, g % 2, 0),
                                          ALU.subtract).then_inc(lo_done, 1)
                    for j in groups[1:]:
                        take_maxes(b, j, base, (0, 1))
                    if has["ln"] and g < 4:
                        layer_norm(b, par, g)
                    if has["att"] and g:
                        norm(b, par, g - 1)
                    if has["last"] and not g:
                        norm(b - 1, 1 - par, NKV - 1)
                    for m, (kind, i) in enumerate(rows[g]):
                        late = (b, par, (k0 + n) % 2, kind, i, base + n + 1)
                        n += 1
                        if m < len(rows[g]) - 1 or g == NKV - 1:
                            split_unit(*late)
                            late = None
                    for j in groups[1:]:
                        take_maxes(b, j, base, (2,))

            steps(dve, step)

        @block.tensor
        def _(pe):
            pe.wait_ge(const_ok, 1)

            def scores(b, par, g, k):
                if g == 0 and k == 0:
                    pe.wait_ge(m_in, 32 * (b + 1))
                K, Q = kst[par], qst[par]
                wait(pe, exp_done, 24 * b + 3 * g + k - 1)
                ps = psT[(g + k) % 2]
                if k < 2:
                    m = pe.matmul(ps[:, 0:2 * S], K[:, g, 0:P], Q[:, 4 * g + 2 * k:4 * g + 2 * k + 2, :],
                                  start=True, stop=True)
                else:
                    m = pe.matmul(ps[0:TXT, 0:REP * TXT], K[:, g, P:S], Q[:, 4 * g:4 * g + 4, P:S],
                                  start=True, stop=True)
                m.then_inc(st_filled, 1)

            def weigh(b, par, g):
                if g == 0:
                    pe.wait_ge(v_in, 32 * (b + 1))
                pe.wait_ge(lo_done, 8 * b + g + 1)
                pe.wait_ge(lo_pool, 16 * b + 2 * g + 2)
                wait(pe, norm_done, 8 * b + g - 1)
                o = psO[g % 2]
                VH, VL = vh[par], vl[par]
                for r in range(REP):
                    def blocks(t):
                        v = view(t, g % 2, r // 2)[:, r % 2, :]
                        return v[:, 0:P], v[:, P:S], view(t, g % 2, 2)[:, r, :]
                    (h00, h01, h11), (l00, l01, l11) = blocks(ph), blocks(pl)
                    first = [(h00, VH, 0), (h00, VL, 0), (l00, VH, 0)]
                    second = [(h01, VH, 0), (h01, VL, 0), (l01, VH, 0), (h11, VH, 1), (h11, VL, 1), (l11, VH, 1)]
                    for t, list_ in enumerate((first, second)):
                        for n, (p, v, j) in enumerate(list_):
                            m = pe.matmul(o[0:T[t], t, r, :], p, v[0:T[j], j, g, :],
                                          start=n == 0, stop=n == len(list_) - 1)
                m.then_inc(av_done, 1)

            def score_rows(b, par, j, k):
                pe.wait_ge(q_in[j // 4], 16 * 12 * (b + 1))
                pe.wait_ge(k_in[j // 4], 16 * 12 * (b + 1))
                K, Q = kst[par], qst[par]
                wait(pe, s_read, 24 * b + 3 * j + k - 1)
                ps = psS[(j + k) % 2]
                if k == 0:
                    pe.matmul(ps[:], ident_bf[:], mask[:], start=True, stop=False, skip_group_check=True)
                    for r in range(REP):
                        m = pe.matmul(ps[:, r * P:(r + 1) * P], Q[0:STACK, 4 * j + r, 0:P], K[0:STACK, j, 0:P],
                                      start=False, stop=r == REP - 1, skip_group_check=True)
                else:
                    v = ps[0:TXT, 0:2 * S].rearrange("p (h i) -> p h i", i=S)
                    pe.matmul(v[:, :, P:S], ident_bf[0:TXT, 0:TXT], mask[0:TXT, 0:2, 0:TXT],
                              start=True, stop=False, skip_group_check=True)
                    for r in range(2):
                        m = pe.matmul(v[:, r, :], Q[0:STACK, 4 * j + 2 * (k - 1) + r, P:S], K[0:STACK, j, :],
                                      start=False, stop=r == 1, skip_group_check=True)
                m.then_inc(s_filled, 1)

            def unit(kind, n, bank, b, par, ks):
                ps, first, last = psJ[bank], ks[0] == 0, ks[-1] == KC - 1
                if kind in "qk":
                    wh, wl = (qh, ql) if kind == "q" else (kh, kl)
                    c = slice(n * P, (n + 1) * P)
                    for k in ks:
                        pe.matmul(ps[:, 0:S], wh[:, k, c], xth[:, par, k, :], start=k == 0, stop=False)
                        pe.matmul(ps[:, 0:S], wh[:, k, c], xtl[:, par, k, :], start=False, stop=False)
                        m = pe.matmul(ps[:, 0:S], wl[:, k, c], xth[:, par, k, :], start=False, stop=k == KC - 1)
                elif kind == "v":
                    r, c = T[n], slice(n * P, n * P + T[n])
                    for k in ks:
                        pe.matmul(ps[0:r, 0:KW], xth[:, par, k, c], kh[:, k, KW:], start=k == 0, stop=False)
                        pe.matmul(ps[0:r, 0:KW], xth[:, par, k, c], kl[:, k, KW:], start=False, stop=False)
                        m = pe.matmul(ps[0:r, 0:KW], xtl[:, par, k, c], kh[:, k, KW:], start=False,
                                      stop=k == KC - 1)
                elif not last:
                    return
                elif kind == "m":
                    pe.wait_ge(s_read, 24 * (b + 2))
                    pe.transpose(ps[0:NH, 0:P], mx[:, 0, :], ident[:])
                    m = pe.transpose(ps[0:NH, P:S], mx[0:TXT, 1, :], ident[0:TXT, 0:TXT])
                else:
                    t, half = divmod(n, 2)
                    pe.wait_ge(ln_done, 2 * (b + 4))
                    r = T[t]
                    for k in range(4):
                        c = 4 * half + k
                        m = pe.transpose(ps[:, k * r:(k + 1) * r], xin[0:r, 1 - par, t, c * P:(c + 1) * P], ident[0:r, 0:r])
                if last:
                    m.then_inc(pj_filled, 1)

            FRONT, BACK = range(KC // 2), range(KC // 2, KC)

            def step(b, par, has):
                base, k0 = before(b, par), odd(b, par)
                rows = units(has)
                n = 0
                for g in SLOTS:
                    groups = MAXES[g] if has["max"] else []

                    def maxes(which, ks):
                        for j in which:
                            for k in ks:
                                score_rows(b + 1, 1 - par, j, k)

                    def project(which, ks):
                        if which < len(rows[g]):
                            kind, m = rows[g][which]
                            if ks is FRONT:
                                wait(pe, pj_lo, base + (n + which - 1))
                            elif n + which == 0:
                                wait(pe, pj_lo, base)
                            unit(kind, m, (k0 + n + which) % 2, b, par, ks)

                    if has["att"]:
                        scores(b, par, g, 0)
                        scores(b, par, g, 1)
                    maxes(groups[:1], (0, 1))
                    project(0, FRONT)
                    if has["att"]:
                        scores(b, par, g, 2)
                    maxes(groups[:1], (2,))
                    project(0, BACK)
                    maxes(groups[1:], (0, 1))
                    if has["att"] and g:
                        weigh(b, par, g - 1)
                    if has["last"] and not g:
                        weigh(b - 1, 1 - par, NKV - 1)
                    maxes(groups[1:], (2,))
                    project(1, FRONT)
                    project(1, BACK)
                    for which in range(2, len(rows[g])):
                        project(which, FRONT)
                        project(which, BACK)
                    n += len(rows[g])

            steps(pe, step)


def rsqrt(dve, chain, rs, var):
    v, y, t, out = (rs[:, k, :] for k in range(4))
    chain(dve.tensor_scalar(v, var, EPS_LN, None, ALU.add))
    chain(dve.tensor_scalar(t.bitcast(I32), v.bitcast(I32), 1, None, ALU.logical_shift_right))
    chain(dve.tensor_scalar(y.bitcast(I32), t.bitcast(I32), -1.0, float(0x5F3759DF), ALU.mult, ALU.add))
    for n in range(3):
        chain(dve.tensor_tensor(t, y, y, ALU.mult))
        chain(dve.scalar_tensor_tensor(t, t, -0.5, v, ALU.mult, ALU.mult))
        chain(dve.scalar_tensor_tensor(out if n == 2 else y, t, 1.5, y, ALU.add, ALU.mult))


def prep_out(nc, stage, staged, cf, mk, enc, in_small, w_base, fourier, woh, wol, wfh, wfl, osc, fsc, ksc):
    HALF, RING = 512, 4
    with ExitStack() as ctx:
        sb = lambda n, s, d=F32: ctx.enter_context(nc.sbuf_tensor(n, s, d))
        sem = lambda n: ctx.enter_context(nc.semaphore(n))
        st = [stage, sb("st_f", [P, KC, D])]
        wb = sb("wb", [P, KC, D])
        fm = sb("fm", [P, RING, D])
        ident = sb("ident4", [P, P])
        mf = [sb("mf0", [P, KC, E, R0]), sb("mf1", [P, KC, E, R1])]
        cm = sb("cm", [P, KC, R])
        gt = sb("gt", [R, D])
        peak, apeak = sb("peak4", [P, 2]), sb("apeak4", [P, 2])
        psG = [ctx.enter_context(nc.psum_tensor(f"psG{i}", [P, HALF], F32)) for i in range(2)]
        psW = [ctx.enter_context(nc.psum_tensor(f"psW{i}", [P, HALF], F32)) for i in range(3)]
        psA = [ctx.enter_context(nc.psum_tensor(f"psA{i}", [P, HALF], F32)) for i in range(3)]
        chunk_peak = sb("chunk_peak", [P, KC])
        s = scale_and_split(nc, ctx, "p4", 2)
        in_b = sem("in_b")
        in_f = [sem(f"in_f{k}") for k in range(KC)]
        cm_ok, id_ok, pool_c, f_used, g_ok, w_filled, a_read, w_read = (sem(n) for n in (
            "cm_ok", "id_ok", "pool_c4", "f_used", "g_ok", "w_filled", "a_read", "w_read"))
        hi, lo, scs, tops = (woh, wfh), (wol, wfl), (osc, fsc), (TOP["o"], TOP["f"])
        block = ctx.enter_context(nc.Block())

        @block.sync
        def _(sp):
            for k in range(KC):
                if k >= RING:
                    sp.wait_ge(f_used, k - RING + 1)
                sp.dma_start(fm[:, k % RING], fourier[k * P:(k + 1) * P, :]).then_inc(in_f[k], 16)
                if k % 4 == 3:
                    c = slice(k - 3, k + 1)
                    sp.dma_start(wb[:, c], w_base.rearrange("(k p) n -> p k n", p=P)[:, c]).then_inc(in_b, 16)

        @block.gpsimd
        def _(pool):
            chain = Chain(pool, pool_c)
            chain(pool.memset(ident[:], 0.0))
            pool.affine_select(out=ident[:], in_=ident[:], compare_op=ALU.not_equal, fill=1.0, base=0,
                               pattern=[[-1, P]], channel_multiplier=1).then_inc(id_ok, 1)
            for n in range(2):
                pool.wait_ge(s["peak"], n + 1)
                pool.partition_all_reduce(apeak[:, n:n + 1], peak[:, n:n + 1], P, RMAX).then_inc(s["all_peak"], 1)

        @block.tensor
        def _(pe):
            pe.wait_ge(in_small, SMALL_LOADS * 16)
            pe.wait_ge(cm_ok, 1)
            for k in range(KC):
                pe.wait_ge(in_f[k], 16)
                for h in range(2):
                    m = pe.matmul(psG[h][0:R, :], cm[:, k, :], fm[:, k % RING, h * HALF:(h + 1) * HALF],
                                  start=k == 0, stop=k == KC - 1)
                m.then_inc(f_used, 1)
            pe.wait_ge(g_ok, 1)
            pe.wait_ge(in_b, 32)
            pe.wait_ge(id_ok, 1)
            for n in range(2 * KC):
                k, h = divmod(n, 2)
                if n >= 3:
                    pe.wait_ge(a_read, n - 2)
                    pe.wait_ge(w_read, n - 2)
                c = slice(k * P, (k + 1) * P)
                pe.matmul(psA[n % 3][:], enc[:, c], gt[:, h * HALF:(h + 1) * HALF], start=True, stop=True)
                for j in range(4):
                    m = pe.transpose(psW[n % 3][:, j * P:(j + 1) * P], wb[:, 4 * h + j, c], ident[:])
                m.then_inc(w_filled, 1)

        @block.scalar
        def _(act):
            for n in range(2):
                if n == 1:
                    for i in range(2 * KC):
                        k, h = divmod(i, 2)
                        act.wait_ge(w_filled, i + 1)
                        act.copy(st[1][:, k, h * HALF:(h + 1) * HALF], psA[i % 3][:]).then_inc(a_read, 1)
                act.wait_ge(s["scale"], n + 1)
                for k in range(KC):
                    act.activation(hi[n][:, k], st[n][:, k], ACT.Copy, scale=scs[n][:, 0:1]).then_inc(s["hi"], 1)

        @block.vector
        def _(dve):
            chain = Chain(dve, s["chain"])
            dve.wait_ge(in_small, SMALL_LOADS * 16)
            for n, (lo_r, hi_r) in enumerate(((0, R0), (R0, R))):
                chain(dve.tensor_copy(mf[n][:], mk[n][:]))
                chain(dve.tensor_tensor(cf[n][:], cf[n][:], mf[n][:], ALU.mult))
                chain(dve.tensor_tensor(mf[n][:, :, 0, :], cf[n][:, :, 0, :], cf[n][:, :, 1, :], ALU.add))
                chain(dve.tensor_tensor(cm[:, :, lo_r:hi_r], mf[n][:, :, 0, :], cf[n][:, :, 2, :], ALU.add))
            dve.sem_inc(cm_ok, 1)

            def find_scale(n):
                dve.wait_ge(s["all_peak"], n + 1)
                weight_scales(dve, chain, apeak[:, n:n + 1], scs[n], tops[n])
                dve.sem_inc(s["scale"], 1)

            def low_parts(n, ks=range(KC)):
                for k in ks:
                    dve.wait_ge(s["hi"], n * KC + k + 1)
                    dve.scalar_tensor_tensor(lo[n][:, k], st[n][:, k], scs[n][:, 0:1], hi[n][:, k],
                                             ALU.mult, ALU.subtract)

            dve.wait_ge(staged, 32)
            dve.tensor_reduce(peak[:, 0:1], st[0][:].rearrange("p k n -> p (k n)"), AX.X, ALU.max,
                              apply_absolute_value=True).then_inc(s["peak"], 1)
            find_scale(0)
            low_parts(0, range(KC // 2))
            dve.wait_ge(f_used, KC)
            for h in range(2):
                m = dve.tensor_scalar(gt[:, h * HALF:(h + 1) * HALF], psG[h][0:R, :], 0.5, None, ALU.mult)
            m.then_inc(g_ok, 1)
            chain(dve.tensor_tensor(osc[:, 2:3], osc[:, 1:2], ksc[:, 1:2], ALU.mult))
            for k in range(KC):
                for h in range(2):
                    n = 2 * k + h
                    half = st[1][:, k, h * HALF:(h + 1) * HALF]
                    dve.wait_ge(a_read, n + 1)
                    dve.tensor_tensor(half, half, psW[n % 3][:], ALU.add).then_inc(w_read, 1)
                if k >= KC // 2:
                    low_parts(0, (k,))
                dve.wait_ge(w_read, 2 * k + 2)
                m = dve.tensor_reduce(chunk_peak[:, k:k + 1], st[1][:, k], AX.X, ALU.max, apply_absolute_value=True)
            chain(m)
            dve.tensor_reduce(peak[:, 1:2], chunk_peak[:], AX.X, ALU.max).then_inc(s["peak"], 1)
            find_scale(1)
            low_parts(1)


def output(nc, hcat, acat, bias, out, woh, wol, wfh, wfl, osc, fsc):
    HALF = 512
    NT = -(-ROWS // P)
    LAST = ROWS - P
    NEW = ROWS - (NT - 1) * P
    with ExitStack() as ctx:
        sb = lambda n, s, d=F32: ctx.enter_context(nc.sbuf_tensor(n, s, d))
        sem = lambda n: ctx.enter_context(nc.semaphore(n))
        ident = sb("ident5", [P, P])
        bias_sb = sb("bias_sb", [P, D])
        a_in = sb("a_in", [P, 2, D])
        h_in = sb("h_in", [P, 2, D])
        h2 = sb("h2", [P, D])
        hb = sb("hb", [P, 2, D])
        xh = sb("xh", [P, D])
        y = sb("y", [P, 2, D])
        ath, atl = sb("ath", [P, KC, P], F16), sb("atl", [P, KC, P], F16)
        xth, xtl = sb("xth5", [P, KC, P], F16), sb("xtl5", [P, KC, P], F16)
        stats, mv, rs = sb("stats5", [P, 2, 6]), sb("mv5", [P, 2]), sb("rs5", [P, 4, 1])
        psT = [ctx.enter_context(nc.psum_tensor(f"ps5T{i}", [P, HALF], F32)) for i in range(4)]
        psO = [ctx.enter_context(nc.psum_tensor(f"ps5O{i}", [P, HALF], F32)) for i in range(2)]
        psF = [ctx.enter_context(nc.psum_tensor(f"ps5F{i}", [P, HALF], F32)) for i in range(2)]
        passed = sem("passed5")
        pool_c, const_ok, bias_in = sem("pool_c5"), sem("const_ok5"), sem("bias_in")
        a_arr = [sem("a_arr0"), sem("a_arr1")]
        h_arr = [sem("h_arr0"), sem("h_arr1")]
        out_ok = [sem("out_ok0"), sem("out_ok1")]
        a_filled, a_hi, a_lo = sem("a_filled"), sem("a_hi"), sem("a_lo")
        x_filled, x_hi, x_lo = sem("x_filled"), sem("x_hi"), sem("x_lo")
        o_filled, o_read, f_filled, f_read = sem("o_filled"), sem("o_read"), sem("f_filled"), sem("f_read")
        ln_c, ln_done, hb_done = sem("ln_c"), sem("ln_done5"), sem("hb_done")

        def parts(t):
            return {"o": 0 <= t < NT, "a": 0 <= t + 1 < NT, "f": 0 <= t - 1 < NT}

        def steps(eng, step):
            for t in range(-1, 2):
                step(t, t % 2, parts(t))
            with eng.Fori(1, NT // 2 - 2) as i:
                step(i * 2, 0, parts(2))
                step(i * 2 + 1, 1, parts(3))
            for t in range(NT - 4, NT + 1):
                step(t, t % 2, parts(t))

        def row(t):
            return LAST if isinstance(t, int) and t == NT - 1 else t * P

        block = ctx.enter_context(nc.Block())

        @block.sync
        def _(sp):
            sp.dma_start(bias_sb[:], bias.rearrange("(o d) -> o d", o=1).broadcast_to([P, D])).then_inc(bias_in, 16)

            def load_a(t, par):
                wait(sp, a_filled, 2 * (t - 1))
                pass_on(sp, passed)
                sp.dma_start(a_in[:, par, :], acat[bass.ds(row(t), P), :]).then_inc(a_arr[par], 16)

            def load_h(t, par):
                wait(sp, o_read, 2 * (t - 1))
                pass_on(sp, passed)
                sp.dma_start(h_in[:, par, :], hcat[bass.ds(row(t), P), :]).then_inc(h_arr[par], 16)

            def store(t, par):
                sp.wait_ge(f_read, 2 * t + 2)
                pass_on(sp, passed)
                if isinstance(t, int) and t == NT - 1:
                    sp.dma_start(out[LAST + P - NEW:ROWS, :], y[P - NEW:P, par, :]).then_inc(out_ok[par], 16)
                else:
                    sp.dma_start(out[bass.ds(t * P, P), :], y[:, par, :]).then_inc(out_ok[par], 16)

            load_a(0, 0)

            def step(t, par, has):
                if has["a"]:
                    load_h(t + 1, 1 - par)
                if not isinstance(t, int) or t + 2 < NT:
                    if not isinstance(t, int) or t + 2 >= 1:
                        load_a(t + 2, par)
                if has["f"]:
                    store(t - 1, 1 - par)

            steps(sp, step)
            for q in out_ok:
                sp.wait_ge(q, 16 * NT // 2)

        @block.gpsimd
        def _(pool):
            chain = Chain(pool, pool_c)
            chain(pool.memset(ident[:], 0.0))
            pool.affine_select(out=ident[:], in_=ident[:], compare_op=ALU.not_equal, fill=1.0, base=0,
                               pattern=[[-1, P]], channel_multiplier=1).then_inc(const_ok, 1)
            pool.wait_ge(bias_in, 16)

            def step(t, par, has):
                if has["o"]:
                    pool.wait_ge(o_read, 2 * t + 2)
                    wait(pool, f_read, 2 * (t - 1))
                    pool.tensor_tensor(hb[:, par, :], h2[:], bias_sb[:], ALU.add).then_inc(hb_done, 1)

            steps(pool, step)

        @block.scalar
        def _(act):
            def split(n, filled, hi_sem, dst, first):
                for h in range(2):
                    act.wait_ge(filled, n + h + 1)
                    act.copy(dst[:, 4 * h:4 * h + 4, :].rearrange("p c j -> p (c j)"),
                             psT[first + h][:]).then_inc(hi_sem, 1)

            def step(t, par, has):
                if has["f"]:
                    split(2 * (t - 1), x_filled, x_hi, xth, 0)
                if has["a"]:
                    split(2 * (t + 1), a_filled, a_hi, ath, 2)

            steps(act, step)

        @block.vector
        def _(dve):
            def split(n, hi_sem, lo_sem, hi, lo, first):
                for h in range(2):
                    dve.wait_ge(hi_sem, n + h + 1)
                    c = slice(4 * h, 4 * h + 4)
                    dve.tensor_tensor(lo[:, c, :].rearrange("p c j -> p (c j)"), psT[first + h][:],
                                      hi[:, c, :].rearrange("p c j -> p (c j)"), ALU.subtract).then_inc(lo_sem, 1)

            LINKS = 15

            def step(t, par, has):
                if has["f"]:
                    split(2 * (t - 1), x_hi, x_lo, xth, xtl, 0)
                if has["o"]:
                    dve.wait_ge(h_arr[par], 8 * (t - par) + 16)
                    wait(dve, hb_done, t)
                    for h in range(2):
                        c = slice(h * HALF, (h + 1) * HALF)
                        dve.wait_ge(o_filled, 2 * t + h + 1)
                        dve.scalar_tensor_tensor(h2[:, c], psO[h][:], osc[:, 2:3], h_in[:, par, c],
                                                 ALU.mult, ALU.add).then_inc(o_read, 1)
                    dve.wait_ge(o_read, 2 * t + 2)
                    chain = Chain(dve, ln_c)
                    chain.base = LINKS * t
                    for h in range(2):
                        chain(dve.bn_stats(stats[:, h, :], h2[:, h * HALF:(h + 1) * HALF]), passed)
                    chain(dve.bn_aggr(mv[:], stats[:]))
                    rsqrt(dve, chain, rs, mv[:, 1:2])
                    assert chain.n == LINKS, chain.n
                    wait(dve, x_filled, 2 * t)
                    dve.tensor_scalar(xh[:], h2[:], mv[:, 0:1], rs[:, 3, :], ALU.subtract, ALU.mult).then_inc(ln_done, 1)
                if has["a"]:
                    split(2 * (t + 1), a_hi, a_lo, ath, atl, 2)
                if has["f"]:
                    dve.wait_ge(hb_done, t)
                    if not isinstance(t, int) or t >= 3:
                        dve.wait_ge(out_ok[1 - par], 8 * (t - 1 - (1 - par)))
                    for h in range(2):
                        c = slice(h * HALF, (h + 1) * HALF)
                        dve.wait_ge(f_filled, 2 * (t - 1) + h + 1)
                        dve.scalar_tensor_tensor(y[:, 1 - par, c], psF[h][:], fsc[:, 1:2], hb[:, 1 - par, c],
                                                 ALU.mult, ALU.add).then_inc(f_read, 1)

            steps(dve, step)

        @block.tensor
        def _(pe):
            pe.wait_ge(const_ok, 1)

            def turn(src, first, filled, lo_sem, n):
                for h in range(2):
                    wait(pe, lo_sem, n - 1 + h)
                    for k in range(4):
                        c = (4 * h + k) * P
                        m = pe.transpose(psT[first + h][:, k * P:(k + 1) * P], src[:, c:c + P], ident[:])
                    m.then_inc(filled, 1)

            def project(ps, th, tl, wh, wl, filled):
                for h in range(2):
                    c = slice(h * HALF, (h + 1) * HALF)
                    for k in range(KC):
                        pe.matmul(ps[h][:], th[:, k, :], wh[:, k, c], start=k == 0, stop=False)
                        pe.matmul(ps[h][:], th[:, k, :], wl[:, k, c], start=False, stop=False)
                        m = pe.matmul(ps[h][:], tl[:, k, :], wh[:, k, c], start=False, stop=k == KC - 1)
                    m.then_inc(filled, 1)

            def step(t, par, has):
                if has["f"]:
                    pe.wait_ge(ln_done, t)
                    turn(xh, 0, x_filled, x_lo, 2 * (t - 1))
                if has["o"]:
                    pe.wait_ge(a_lo, 2 * t + 2)
                    wait(pe, o_read, 2 * t)
                    project(psO, ath, atl, woh, wol, o_filled)
                if has["a"]:
                    pe.wait_ge(a_arr[1 - par], 8 * (t + 1 - (1 - par)) + 16)
                    turn(a_in[:, 1 - par, :], 2, a_filled, a_lo, 2 * (t + 1))
                if has["f"]:
                    pe.wait_ge(x_lo, 2 * t)
                    wait(pe, f_read, 2 * (t - 1))
                    project(psF, xth, xtl, wfh, wfl, f_filled)

            steps(pe, step)


def build(nc, x, txt, log_dt, lam, wq, wk, wv, wo, w_base, b_base, enc0, enc1, coefs0, coefs1, mask0, mask1,
          fourier, out, hcat, acat):
    with ExitStack() as ctx:
        sb = lambda n, s, d=F16: ctx.enter_context(nc.sbuf_tensor(n, s, d))
        staged = ctx.enter_context(nc.semaphore("staged"))
        in_small = ctx.enter_context(nc.semaphore("in_small_weights"))
        ksc = sb("ksc", [P, 4], F32)
        stage = sb("stage", [P, KC, D], F32)
        by_chunk = lambda w: w.rearrange("(k p) n -> p k n", p=P)
        peak = sb("peak_q", [P, 1], F32)
        ssm(nc, x, txt, log_dt, lam, hcat, (stage[:], by_chunk(wq), staged), peak)
        cf = [sb("cf0", [P, KC, E, R0], F32), sb("cf1", [P, KC, E, R1], F32)]
        mk = [sb("mk0", [P, KC, E, R0], I32), sb("mk1", [P, KC, E, R1], I32)]
        enc = sb("enc", [R, D], F32)
        with ExitStack() as inner:
            sb3 = lambda n, s, d=F16: inner.enter_context(nc.sbuf_tensor(n, s, d))
            qh, ql = sb3("qh", [P, KC, QW]), sb3("ql", [P, KC, QW])
            kh, kl = sb3("kh", [P, KC, 2 * KW]), sb3("kl", [P, KC, 2 * KW])
            qsc, escale = sb3("qsc", [P, 4], F32), sb3("escale", [P, 1], F32)
            prep_qkv(nc, stage, peak, wk, wv, qh, ql, kh, kl, qsc, ksc, escale)
            ahead = [(stage[:], by_chunk(wo), staged), (enc[0:R0, :], enc0, in_small), (enc[R0:R, :], enc1, in_small)]
            for n, (c, m) in enumerate(((coefs0, mask0), (coefs1, mask1))):
                for e in range(E):
                    ahead.append((cf[n][:, :, e, :], by_chunk(c[e]), in_small))
                    ahead.append((mk[n][:, :, e, :], by_chunk(m[e]), in_small))
            attention(nc, ahead, hcat, acat, qh, ql, kh, kl, escale)
        osc, fsc = sb("osc", [P, 4], F32), sb("fsc", [P, 4], F32)
        with ExitStack() as inner:
            woh, wol, wfh, wfl = (sb(n, [P, KC, D]) for n in ("woh", "wol", "wfh", "wfl"))
            prep_out(nc, stage, staged, cf, mk, enc, in_small, w_base, fourier,
                     woh, wol, wfh, wfl, osc, fsc, ksc)
            output(nc, hcat, acat, b_base, out, woh, wol, wfh, wfl, osc, fsc)


def fourier_matrix(n):
    o = np.arange(n, dtype=np.float64)
    m = np.zeros((n, n))
    m[0] = 1.0 / np.sqrt(n)
    for k in range(1, (n - 1) // 2 + 1):
        m[2 * k - 1] = np.sqrt(2.0 / n) * np.cos(2 * np.pi * ((k * o) % n) / n)
        m[2 * k] = np.sqrt(2.0 / n) * np.sin(2 * np.pi * ((k * o) % n) / n)
    m[n - 1] = (1.0 - 2.0 * (o % 2)) / np.sqrt(n)
    return m.astype(np.float32)


_INS = ["x", "txt", "L0_tok_log_dt", "L0_tok_Lambda", "L0_attn_wq", "L0_attn_wk", "L0_attn_wv", "L0_attn_wo",
        "L0_ffn_W_base", "L0_ffn_b_base", "L0_ffn_enc0", "L0_ffn_enc1", "L0_ffn_coefs0", "L0_ffn_coefs1",
        "L0_ffn_mask0", "L0_ffn_mask1"]


def kernel(**inputs):
    import concourse.bacc as bacc
    from concourse.bass_utils import run_bass_kernel_spmd

    nc = bacc.Bacc("TRN2", target_bir_lowering=False, num_devices=1)
    arrays, args = {}, []
    for name in _INS:
        a = np.ascontiguousarray(inputs[name])
        if a.dtype == np.bool_:
            a = a.astype(np.int32)
        arrays[f"in_{name}"] = a
        args.append(nc.dram_tensor(f"in_{name}", a.shape, mybir.dt.from_np(a.dtype), kind="ExternalInput").ap())
    arrays["in_fourier"] = fourier_matrix(D)
    args.append(nc.dram_tensor("in_fourier", (D, D), F32, kind="ExternalInput").ap())
    args.append(nc.dram_tensor("out_0", (ROWS, D), F32, kind="ExternalOutput").ap())
    args.append(nc.dram_tensor("hcat", (ROWS, D), F32, kind="Internal").ap())
    args.append(nc.dram_tensor("acat", (ROWS, D), F32, kind="Internal").ap())
    build(nc, *args)
    r = run_bass_kernel_spmd(nc, [arrays], core_ids=[0])
    return r.results[0]["out_0"].reshape(B, S, D)
```
